# Optimizing a Trainium2 kernel written in Bass

```python
import numpy as np
import jax
import jax.numpy as jnp

def _softmax(x, axis=-1):
    return jax.nn.softmax(x, axis=axis)
def _gelu(x):
    return jax.nn.gelu(x, approximate=True)
def _silu(x):
    return jax.nn.silu(x)
def _sigmoid(x):
    return jax.nn.sigmoid(x)
def _layernorm(x, axis=-1, eps=1e-5):
    m = jnp.mean(x, axis=axis, keepdims=True)
    v = jnp.var(x, axis=axis, keepdims=True)
    return (x - m) / jnp.sqrt(v + eps)
def _scatter_add(tgt, idx, src, axis=0):
    return tgt.at[idx].add(src)
def _segment_sum(src, seg, n):
    return jax.ops.segment_sum(src, seg, n)

kernel_name = 'mk_adj_preln_d2_adj_512_702b9b'

def setup_inputs(seed: int = 0):
    np.random.seed(seed)
    _w = jnp.asarray
    def _rec_inputs():
        import jax
        import jax.numpy as jnp
        _gk = jax.random.key(seed)
        x = -0.0002928 + 1 * jax.random.normal(jax.random.fold_in(_gk, 1), (4096, 512), jnp.float32)
        _w = (1.0 + jnp.arange(4096, dtype=jnp.float32)) ** -0.5
        _w = _w / _w.mean()
        _pij = jnp.clip(0.00195312 * _w[:, None] * _w[None, :], 0.0, 1.0)
        _a = jax.random.uniform(jax.random.fold_in(_gk, 2), (4096, 4096)) < _pij
        _af = _a.astype(jnp.float32)
        adj = _af
        return x, adj
    x, adj = _rec_inputs()
    def _L0_gnn_setup():
        import jax, jax.numpy as jnp
        import numpy as np
        N = 8192
        D_IN = 512
        D_OUT = 512
        NEG_BIG = -9000000000000000.0
        key = jax.random.key(seed)
        kx, ka, kw, kb, kn, ke = jax.random.split(key, 6)
        x = jax.random.normal(kx, (N, D_IN), dtype=jnp.float32)
        adj = (jax.random.uniform(ka, (N, N)) > 0.9).astype(jnp.float32)
        stdv = 1.0 / np.sqrt(D_OUT)
        weight = jax.random.uniform(kw, (D_IN, D_OUT), minval=-stdv, maxval=stdv, dtype=jnp.float32)
        bias = jax.random.uniform(kb, (D_OUT,), minval=-stdv, maxval=stdv, dtype=jnp.float32)
        node_w = jax.random.uniform(kn, (D_IN, 1), minval=-1.0, maxval=1.0, dtype=jnp.float32)
        stdv_e = 1.0 / np.sqrt(D_IN)
        edge_w = jax.random.uniform(ke, (D_IN, D_IN), minval=-stdv_e, maxval=stdv_e, dtype=jnp.float32)
        return {'x': x, 'adj': adj, 'weight': weight, 'bias': bias, 'node_w': node_w, 'edge_w': edge_w}
    _L0_gnn_all = _L0_gnn_setup()
    _L0_gnn_in = {k: v for k, v in _L0_gnn_all.items() if k in ('weight', 'bias', 'node_w', 'edge_w', )}
    del _L0_gnn_all

    def _L1_gnn_setup():
        import jax, jax.numpy as jnp
        import numpy as np
        key = jax.random.key(seed)
        k1, k2, k3 = jax.random.split(key, 3)
        N, D_in, D_out = (8192, 512, 512)
        features = jax.random.normal(k1, (N, D_in), dtype=jnp.float32)
        adj = jax.random.uniform(k2, (N, N), dtype=jnp.float32)
        limit = float(np.sqrt(6.0 / (D_in + D_out)))
        weight = jax.random.uniform(k3, (D_in, D_out), dtype=jnp.float32, minval=-limit, maxval=limit)
        return {'features': features, 'adj': adj, 'weight': weight}
    _L1_gnn_all = _L1_gnn_setup()
    _L1_gnn_in = {k: v for k, v in _L1_gnn_all.items() if k in ('weight', )}
    del _L1_gnn_all

    return {
        "x": x,
        "adj": adj,
        "L0_gnn_weight": _L0_gnn_in["weight"],
        "L0_gnn_bias": _L0_gnn_in["bias"],
        "L0_gnn_node_w": _L0_gnn_in["node_w"],
        "L0_gnn_edge_w": _L0_gnn_in["edge_w"],
        "L1_gnn_weight": _L1_gnn_in["weight"],
    }

def reference(x, adj, L0_gnn_weight, L0_gnn_bias, L0_gnn_node_w, L0_gnn_edge_w, L1_gnn_weight):
    import jax
    import jax.numpy as jnp
    def _L0_gnn_ref(x, adj, weight, bias, node_w, edge_w):
        import jax, jax.numpy as jnp
        import numpy as np
        N = 8192
        D_IN = 512
        D_OUT = 512
        NEG_BIG = -9000000000000000.0
        node_att = jax.nn.softmax(x @ node_w, axis=0)
        h = x @ edge_w
        e = h @ h.T
        e = jnp.where(adj > 0, e, NEG_BIG)
        edge_att = jax.nn.softmax(e, axis=1)
        combined_att = node_att * edge_att
        support = x @ weight
        output = adj * combined_att @ support
        return output + bias

    def _L1_gnn_ref(features, adj, weight):
        import jax, jax.numpy as jnp
        import numpy as np
        agg = jnp.matmul(adj, features)
        x = jnp.matmul(agg, weight)
        return jax.nn.relu(x)

    h = jnp.maximum(_layernorm(x, axis=-1), 0.0)
    x = x + _L0_gnn_ref(h, adj, L0_gnn_weight, L0_gnn_bias, L0_gnn_node_w, L0_gnn_edge_w)
    h = jnp.maximum(_layernorm(x, axis=-1), 0.0)
    x = x + _L1_gnn_ref(h, adj, L1_gnn_weight)
    return x


_drawn_inputs = setup_inputs


def setup_inputs(seed=0):
    import zlib

    import numpy as np

    out = dict(_drawn_inputs(seed))
    spreads = {}
    factors = {'L0_gnn_weight': 29.767, 'L0_gnn_node_w': 28.863, 'L0_gnn_edge_w': 35.327}
    for name, (base, spread) in spreads.items():
        noise = np.random.default_rng([zlib.crc32(name.encode()), seed]).standard_normal(out[name].shape)
        drawn = base * np.exp(spread * noise) if base else spread * noise
        out[name] = jnp.asarray(drawn.astype(out[name].dtype))
    for name, factor in factors.items():
        out[name] = (out[name] * factor).astype(out[name].dtype)
    return out
```

```python
from contextlib import ExitStack

import concourse.bass as bass
from concourse import mybir
import numpy as np

P = 128
N, D = 4096, 512
TILES = N // P
KD = D // P
CW = 512
CHUNKS = N // CW
BPC = CW // P
GT = 4
GROUPS = TILES // GT
EPS = 1e-5
NEG_BIG = -9000000000000000.0

H_SCALE = 64.0
W_SCALE = 64.0
G_SCALE = 8.0
S_SCALE = 16.0
P_SCALE = 256.0
Y_SCALE = 64.0
E_SCALE = G_SCALE * G_SCALE


def wait_from(engine, semaphore, value):
    if isinstance(value, int) and value <= 0:
        return
    engine.wait_ge(semaphore, value)


def build_program(nc, x, adj, weight, bias, node_w, edge_w, weight1, out):
    f32, f16 = mybir.dt.float32, mybir.dt.float16
    ALU, ACT, AX = mybir.AluOpType, mybir.ActivationFunctionType, mybir.AxisListType

    adjT_dram = nc.dram_tensor("adjT_scratch", (TILES, P, N), f16, kind="Internal").ap()
    y_dram = nc.dram_tensor("y_scratch", (TILES, P, 2, D), f16, kind="Internal").ap()
    x1_dram = nc.dram_tensor("x1_scratch", (TILES, P, D), f32, kind="Internal").ap()

    x_groups = x.rearrange("(g t p) d -> g p t d", t=GT, p=P)
    x_tiles = x.rearrange("(t p) d -> t p d", p=P)
    adj_tiles = adj.rearrange("(t p) n -> t p n", p=P)
    out_tiles = out.rearrange("(t p) d -> t p d", p=P)

    with ExitStack() as ctx:
        def sb(name, shape, dt):
            return ctx.enter_context(nc.sbuf_tensor(name, shape, dt))

        def sem(name):
            return ctx.enter_context(nc.semaphore(name))

        gT_hi = sb("gT_hi", [P, KD, N], f16)
        gT_lo = sb("gT_lo", [P, KD, N], f16)
        s_hi = sb("s_hi", [P, TILES, D], f16)
        s_lo = sb("s_lo", [P, TILES, D], f16)
        probs = sb("probs", [P, N], f32)
        adj_sb = sb("adj_sb", [P, 2, N], f32)
        w1_hl = sb("w1_hl", [P, 2, KD, D], f16)
        shared = sb("shared", [P, 8192], f16)
        g_cur = sb("g_cur", [P, 2, KD, P], f16)
        x_sb = sb("x_sb", [P, D], f32)
        x1_sb = sb("x1_sb", [P, D], f32)
        h1_sb = sb("h1_sb", [P, D], f32)
        h1T = sb("h1T", [P, 2, KD, P], f16)
        y_out = sb("y_out", [P, 2, D], f16)
        bias_sb = sb("bias_sb", [P, D], f32)
        ident = sb("ident", [P, P], f32)
        ones = sb("ones", [P, P], f32)
        half = sb("half", [P, GT], f32)
        node_f = sb("node_f", [P, KD], f32)
        node_hl = sb("node_hl", [P, 2, KD], f16)
        logits = sb("logits", [P, TILES], f32)
        node_att = sb("node_att", [P, TILES], f32)
        node_col = sb("node_col", [P, 1], f32)
        node_neg = sb("node_neg", [P, 1], f32)
        node_sum = sb("node_sum", [P, 1], f32)
        node_rec = sb("node_rec", [P, 1], f32)
        node_row = sb("node_row", [P, P], f32)
        stats = sb("stats", [P, GT, 6], f32)
        moments = sb("moments", [P, GT, 2], f32)
        var_eps = sb("var_eps", [P, GT], f32)
        rough = sb("rough", [P, GT], f32)
        newton = sb("newton", [P, GT], f32)
        rstd = sb("rstd", [P, GT], f32)
        chunk_max = sb("chunk_max", [P, CHUNKS], f32)
        row_max = sb("row_max", [P, 1], f32)
        neg_max = sb("neg_max", [P, 1], f32)
        chunk_sum = sb("chunk_sum", [P, 2, CHUNKS], f32)
        row_sum = sb("row_sum", [P, 1], f32)
        row_rec = sb("row_rec", [P, 1], f32)
        row_fac = sb("row_fac", [P, 1], f32)

        edge_hl = shared[:, 0:4096].rearrange("p (h k n) -> p h k n", h=2, k=KD)
        w_hl = shared[:, 4096:8192].rearrange("p (h k n) -> p h k n", h=2, k=KD)
        hT = probs[:, :].bitcast(f16).rearrange("p (s h k n) -> p s h k n", s=2, h=2, k=KD)
        xg = adj_sb[:, 0, :].rearrange("p (s t d) -> p s t d", s=2, t=GT)
        hg = adj_sb[:, 1, :].rearrange("p (s t d) -> p s t d", s=2, t=GT)
        stage_edge = s_lo[:, 24:32, :].rearrange("p a b -> p (a b)").bitcast(f32)
        stage_w = s_hi[:, 24:32, :].rearrange("p a b -> p (a b)").bitcast(f32)
        stage_w1 = s_hi[:, 16:24, :].rearrange("p a b -> p (a b)").bitcast(f32)
        penalty = shared[:, 0:2048].bitcast(f32).rearrange("p (s n) -> p s n", s=2)
        pT_hi = shared[:, 2048:4096].rearrange("p (s b n) -> p s b n", s=4, b=BPC)
        pT_lo = shared[:, 4096:6144].rearrange("p (s b n) -> p s b n", s=4, b=BPC)
        adjT_sb = shared[:, 6144:8192].rearrange("p (s n) -> p s n", s=2)
        y_hi = gT_hi[:, :, :].rearrange("p k n -> p (k n)").rearrange("p (j d) -> p j d", d=D)
        y_lo = gT_lo[:, :, :].rearrange("p k n -> p (k n)").rearrange("p (j d) -> p j d", d=D)
        adjT_grp = [adj_sb[:, :, :].rearrange("p s n -> p (s n)").bitcast(f16).rearrange("p (t n) -> p t n", t=GT),
                    s_hi[:, :, :].rearrange("p j d -> p (j d)").rearrange("p (t n) -> p t n", t=GT)]
        x1_grp = probs[:, :].rearrange("p (s t d) -> p s t d", s=2, t=GT)
        out_grp = s_lo[:, :, :].rearrange("p j d -> p (j d)").bitcast(f32).rearrange(
            "p (s t d) -> p s t d", s=4, t=GT)

        banks = ctx.enter_context(nc.psum_tensor("banks", [P, 8, 512], f32))
        hT_ps = [banks[:, b, :] for b in (0, 1)]
        g_ps = [banks[:, b, :] for b in (2, 3)]
        s_ps = [banks[:, b, :] for b in (4, 5)]
        node_ps = banks[:, 6, :]
        score_ps = [banks[:, b, :] for b in (0, 1)]
        pT_ps = [banks[:, b, :] for b in (2, 3)]
        adjT_ps = banks[:, 4, :]
        att_ps = banks[:, 5, :]
        h1T_ps = banks[:, 6, :]
        y_ps = banks[:, 7, :]

        ident_made = sem("ident_made")
        ones_made = sem("ones_made")
        edge_in = sem("edge_in")
        weight_in = sem("weight_in")
        w1_in = sem("w1_in")
        node_in = sem("node_in")
        bias_in = sem("bias_in")
        w_hi_made = sem("w_hi_made")
        w_lo_made = sem("w_lo_made")
        xg_in = [sem("xg_in0"), sem("xg_in1")]
        stats_made = sem("stats_made")
        var_made = sem("var_made")
        rough_made = sem("rough_made")
        h_made = sem("h_made")
        hT_done = sem("hT_done")
        hT_hi_made = sem("hT_hi_made")
        hT_lo_made = sem("hT_lo_made")
        g_done = sem("g_done")
        g_hi_made = sem("g_hi_made")
        g_lo_made = sem("g_lo_made")
        s_done = sem("s_done")
        s_hi_made = sem("s_hi_made")
        s_lo_made = sem("s_lo_made")
        node_done = sem("node_done")
        logits_made = sem("logits_made")
        node_step = sem("node_step")
        node_row_done = sem("node_row_done")
        node_exp_made = sem("node_exp_made")
        node_total_done = sem("node_total_done")
        adj_in = [[sem("adj_in00"), sem("adj_in01")], [sem("adj_in10"), sem("adj_in11")]]
        x_in = sem("x_in")
        xb_made = sem("xb_made")
        g_cur_made = sem("g_cur_made")
        penalty_made = sem("penalty_made")
        score_done = sem("score_done")
        masked = sem("masked")
        max_step = sem("max_step")
        exp_made = sem("exp_made")
        probs_made = sem("probs_made")
        pT_done = sem("pT_done")
        pT_hi_made = sem("pT_hi_made")
        pT_lo_made = sem("pT_lo_made")
        att_done = sem("att_done")
        adjT_done = sem("adjT_done")
        adjT_made = sem("adjT_made")
        adjT_out = [sem("adjT_out0"), sem("adjT_out1")]
        sum_step = sem("sum_step")
        x1_made = sem("x1_made")
        x1_out = sem("x1_out")
        h1_made = sem("h1_made")
        h1T_done = sem("h1T_done")
        h1T_hi_made = sem("h1T_hi_made")
        h1T_lo_made = sem("h1T_lo_made")
        y_done = sem("y_done")
        y_hi_made = sem("y_hi_made")
        y_lo_made = sem("y_lo_made")
        y_stored = sem("y_stored")
        Y_LOADS = [(0, 16), (16, 28), (28, 31), (31, 32)]
        y_in = [sem(f"y_in{n}") for n in range(len(Y_LOADS))]
        adjT_in = [sem("adjT_in0"), sem("adjT_in1")]
        x1_in = [sem("x1_in0"), sem("x1_in1")]
        z_done = sem("z_done")
        relu_made = sem("relu_made")
        out_made = sem("out_made")
        out_stored = [sem("out_stored0"), sem("out_stored1")]

        block = ctx.enter_context(nc.Block())

        def steps(engine, body):
            body(0)
            body(1)
            with engine.Fori(0, (TILES - 2) // 2) as s:
                body(s * 2 + 2, parity=0)
                body(s * 2 + 3, parity=1)
            body(TILES)
            body(TILES + 1)

        def parts(i, parity):
            if isinstance(i, int):
                return i < TILES, 1 <= i <= TILES, i >= 2, i % 2
            return True, True, True, parity

        @block.sync
        def _(sp):
            sp.dma_start(xg[:, 0], x_groups[0]).then_inc(xg_in[0], 16)
            sp.dma_start(stage_edge.rearrange("p (k n) -> p k n", k=KD),
                         edge_w.rearrange("(k p) n -> p k n", p=P)).then_inc(edge_in, 16)
            sp.dma_start(xg[:, 1], x_groups[1]).then_inc(xg_in[1], 16)
            sp.dma_start(stage_w.rearrange("p (k n) -> p k n", k=KD),
                         weight.rearrange("(k p) n -> p k n", p=P)).then_inc(weight_in, 16)
            with nc.allow_non_contiguous_dma(reason="512 words, once"):
                sp.dma_start(node_f[:, :], node_w.rearrange("(k p) o -> p (k o)", p=P)).then_inc(node_in, 16)
            sp.dma_start(stage_w1.rearrange("p (k n) -> p k n", k=KD),
                         weight1.rearrange("(k p) n -> p k n", p=P)).then_inc(w1_in, 16)
            sp.dma_start(bias_sb[:, :], bias.rearrange("(o n) -> o n", o=1).to_broadcast((P, D))).then_inc(bias_in, 16)
            with sp.Fori(0, (GROUPS - 2) // 2) as s:
                for half_ in range(2):
                    g = s * 2 + half_
                    sp.wait_ge(h_made, g * GT + GT)
                    sp.dma_start(xg[:, half_], x_groups[bass.ds(g + 2, 1)].rearrange("o p t d -> (o p) t d")
                                 ).then_inc(xg_in[half_], 16)

            def load_adj(i, slot):
                for hf in range(2):
                    sp.dma_start(adj_sb[:, slot, hf * 2048:(hf + 1) * 2048],
                                 adj_tiles[bass.ds(i, 1), :, hf * 2048:(hf + 1) * 2048].rearrange("o p n -> (o p) n")
                                 ).then_inc(adj_in[slot][hf], 16)

            def load_x(i):
                sp.dma_start(x_sb[:, :], x_tiles[bass.ds(i, 1)].rearrange("o p d -> (o p) d")).then_inc(x_in, 16)

            sp.wait_ge(h_made, TILES)
            load_adj(0, 0)
            load_x(0)

            def step(i, parity=0):
                scores, products, layer1, par = parts(i, parity)
                if layer1:
                    sp.wait_ge(x1_made, i - 1)
                    sp.dma_start(x1_dram[bass.ds(i - 2, 1)].rearrange("o p d -> (o p) d"), x1_sb[:, :]).then_inc(x1_out, 16)
                    if products:
                        load_x(i - 1)
                if scores:
                    if isinstance(i, int) and i == 0:
                        sp.wait_ge(hT_done, GROUPS * KD)
                        load_adj(1, 1)
                    elif not (isinstance(i, int) and i == TILES - 1):
                        sp.wait_ge(probs_made, i * CHUNKS)
                        sp.wait_ge(adjT_done, i * CHUNKS)
                        load_adj(i + 1, 1 - par)
                if layer1:
                    store_y(i - 2)

            def store_y(y):
                sp.wait_ge(y_lo_made, y + 1)
                sp.dma_start(y_dram[bass.ds(y, 1)].rearrange("o p h d -> (o p) h d"), y_out[:, :, :]).then_inc(y_stored, 16)

            step(0)
            step(1)
            with sp.Fori(0, (TILES - 4) // 2) as s:
                step(s * 2 + 2, parity=0)
                step(s * 2 + 3, parity=1)
            step(TILES - 2)
            step(TILES - 1)

            def load_y(n):
                a, b = Y_LOADS[n]
                for hl, to in ((0, y_hi), (1, y_lo)):
                    sp.dma_start(to[:, a:b, :], y_dram[a:b, :, hl, :].rearrange("j p d -> p j d")).then_inc(y_in[n], 16)

            def load_adjT(G, slot):
                sp.dma_start(adjT_grp[slot], adjT_dram[bass.ds(G * GT, GT)].rearrange("t p n -> p t n")).then_inc(adjT_in[slot], 16)

            def load_x1(G, slot):
                sp.dma_start(x1_grp[:, slot], x1_dram[bass.ds(G * GT, GT)].rearrange("t p d -> p t d")).then_inc(x1_in[slot], 16)

            sp.wait_ge(score_done, TILES * CHUNKS)
            sp.wait_ge(y_stored, 28 * 16)
            load_y(0)
            load_y(1)
            sp.wait_ge(probs_made, TILES * CHUNKS)
            for sl in range(2):
                sp.wait_ge(adjT_out[sl], TILES * 2 * 16)
            load_adjT(0, 0)
            step(TILES)
            sp.wait_ge(y_stored, 31 * 16)
            load_y(2)
            sp.wait_ge(pT_done, TILES * CHUNKS)
            sp.wait_ge(x1_out, 31 * 16)
            load_x1(0, 0)
            load_x1(1, 1)
            sp.wait_ge(att_done, TILES * CHUNKS)
            load_adjT(1, 1)
            step(TILES + 1)
            sp.wait_ge(y_stored, TILES * 16)
            load_y(3)
            sp.wait_ge(x1_out, TILES * 16)

            def group(G, slot, ahead):
                if ahead:
                    sp.wait_ge(z_done, G * GT + GT)
                    load_adjT(G + 2, slot)
                for t in range(GT):
                    sp.wait_ge(out_made, G * GT + t + 1)
                    sp.dma_start(out_tiles[bass.ds(G * GT + t, 1)].rearrange("o p d -> (o p) d"),
                                 out_grp[:, slot, t]).then_inc(out_stored[slot], 16)
                if ahead:
                    load_x1(G + 2, slot)

            with sp.Fori(0, GROUPS // 2 - 1) as s:
                group(s * 2, 0, True)
                group(s * 2 + 1, 1, True)
            group(GROUPS - 2, 0, False)
            group(GROUPS - 1, 1, False)
            for sl in range(2):
                sp.wait_ge(out_stored[sl], GROUPS // 2 * GT * 16)

        @block.gpsimd
        def _(pool):
            nc.gpsimd.memset(ident[:, :], 0.0).then_inc(ident_made, 1)
            pool.wait_ge(ident_made, 1)
            nc.gpsimd.affine_select(out=ident[:, :], in_=ident[:, :], compare_op=ALU.not_equal, fill=1.0,
                                    base=0, pattern=[[-1, P]], channel_multiplier=1).then_inc(ident_made, 1)
            nc.gpsimd.memset(half[:, :], -0.5).then_inc(ones_made, 1)
            nc.gpsimd.memset(ones[:, :], 1.0).then_inc(ones_made, 1)
            pool.wait_ge(ones_made, 2)
            with pool.Fori(0, GROUPS) as g:
                pool.wait_ge(var_made, g + 1)
                nc.gpsimd.tensor_tensor(rough[:, :], var_eps[:, :], half[:, :], ALU.pow).then_inc(rough_made, 1)
            pool.wait_ge(bias_in, 16)

            def copy_g(i):
                for hl, src in ((0, gT_hi), (1, gT_lo)):
                    nc.gpsimd.tensor_copy(g_cur[:, hl], src[:, :, bass.ds(i * P, P)]).then_inc(g_cur_made, 1)

            pool.wait_ge(g_lo_made, GROUPS * KD)
            pool.wait_ge(g_hi_made, GROUPS * KD)
            copy_g(0)

            def step(i, parity=0):
                scores, products, layer1, par = parts(i, parity)
                if layer1:
                    pool.wait_ge(var_made, i - 1 + GROUPS)
                    nc.gpsimd.tensor_tensor(rough[:, 0:1], var_eps[:, 0:1], half[:, 0:1], ALU.pow).then_inc(rough_made, 1)
                if products:
                    pool.wait_ge(x_in, i * 16)
                    nc.gpsimd.tensor_tensor(x_sb[:, :], x_sb[:, :], bias_sb[:, :], ALU.add).then_inc(xb_made, 1)
                if scores and not (isinstance(i, int) and i == TILES - 1):
                    pool.wait_ge(score_done, i * CHUNKS + CHUNKS)
                    copy_g(i + 1)

            step(0)
            step(1)
            with pool.Fori(0, (TILES - 4) // 2) as s:
                step(s * 2 + 2, parity=0)
                step(s * 2 + 3, parity=1)
            step(TILES - 2)
            step(TILES - 1)
            step(TILES)
            step(TILES + 1)

        @block.scalar
        def _(act):
            def hi_of_weight(to, src, arrived):
                act.wait_ge(arrived, 16)
                nc.scalar.activation(to, src, ACT.Copy, scale=W_SCALE).then_inc(w_hi_made, 1)

            hi_of_weight(edge_hl[:, 0].rearrange("p k n -> p (k n)"), stage_edge, edge_in)
            hi_of_weight(w_hl[:, 0].rearrange("p k n -> p (k n)"), stage_w, weight_in)
            hi_of_weight(node_hl[:, 0], node_f[:, :], node_in)

            def hT_hi(g, k, slot):
                act.wait_ge(hT_done, g * KD + k + 1)
                wait_from(act, node_done, g - 1)
                nc.scalar.activation(hT[:, slot, 0, k], hT_ps[k % 2], ACT.Relu).then_inc(hT_hi_made, 1)

            def project(g, slot, ahead):
                for m in range(KD):
                    if ahead:
                        hT_hi(g + 1, m, 1 - slot)
                    act.wait_ge(g_done, g * KD + m + 1)
                    nc.scalar.activation(gT_hi[:, m, bass.ds(g * CW, CW)], g_ps[m % 2], ACT.Copy,
                                         scale=G_SCALE / (H_SCALE * W_SCALE)).then_inc(g_hi_made, 1)
                for t in range(GT):
                    act.wait_ge(s_done, g * GT + t + 1)
                    nc.scalar.activation(s_hi[:, bass.ds(g * GT + t, 1)].rearrange("p o d -> p (o d)"), s_ps[t % 2],
                                         ACT.Copy, scale=S_SCALE / (H_SCALE * W_SCALE)).then_inc(s_hi_made, 1)

            for k in range(KD):
                hT_hi(0, k, 0)
            hi_of_weight(w1_hl[:, 0].rearrange("p k n -> p (k n)"), stage_w1, w1_in)
            project(0, 0, True)
            with act.Fori(0, (GROUPS - 2) // 2) as s:
                project(s * 2 + 1, 1, True)
                project(s * 2 + 2, 0, True)
            project(GROUPS - 1, 1, False)

            def store_adjT(i, pair):
                act.wait_ge(adjT_made, i * CHUNKS + 2 * pair + 2)
                act.dma_start(adjT_dram[bass.ds(i, 1), :, pair * 1024:(pair + 1) * 1024].rearrange("o p n -> (o p) n"),
                              adjT_sb[:, pair % 2, :]).then_inc(adjT_out[pair % 2], 16)

            def step(i, parity=0):
                scores, products, layer1, par = parts(i, parity)
                first = isinstance(i, int) and i == 0
                for c in range(CHUNKS):
                    if scores and c in (2, 4, 6):
                        store_adjT(i, c // 2 - 1)
                    if products:
                        n = (i - 1) * CHUNKS + c
                        act.wait_ge(pT_done, n + 1)
                        wait_from(act, att_done, n - 3)
                        nc.scalar.activation(pT_hi[:, c % 4].rearrange("p b n -> p (b n)"), pT_ps[c % 2], ACT.Copy,
                                             scale=P_SCALE).then_inc(pT_hi_made, 1)
                    if scores:
                        act.wait_ge(adjT_done, i * CHUNKS + c + 1)
                        if c % 2 == 0:
                            wait_from(act, adjT_out[(c // 2) % 2], (i * 2 + c // 4) * 16)
                        nc.scalar.activation(adjT_sb[:, (c // 2) % 2, (c % 2) * CW:(c % 2 + 1) * CW], adjT_ps,
                                             ACT.Copy).then_inc(adjT_made, 1)
                    if layer1 and c == 3:
                        act.wait_ge(h1T_done, i - 1)
                        nc.scalar.activation(h1T[:, 0].rearrange("p k n -> p (k n)"), h1T_ps, ACT.Relu).then_inc(h1T_hi_made, 1)
                    if layer1 and c == 6:
                        act.wait_ge(y_done, i - 1)
                        wait_from(act, y_stored, (i - 2) * 16)
                        nc.scalar.activation(y_out[:, 0], y_ps, ACT.Copy,
                                             scale=Y_SCALE / (H_SCALE * W_SCALE)).then_inc(y_hi_made, 1)
                    if first and c == 4:
                        act.wait_ge(node_step, 3)
                        nc.scalar.activation(node_att[:, :], logits[:, :], ACT.Exp, bias=node_neg[:, :],
                                             accum_out=node_sum[:, :]).then_inc(node_exp_made, 1)
                if scores:
                    store_adjT(i, CHUNKS // 2 - 1)
                    act.wait_ge(max_step, i * 2 + 2)
                    for c in range(CHUNKS):
                        row = probs[:, c * CW:(c + 1) * CW]
                        nc.scalar.activation(row, row, ACT.Exp, bias=neg_max[:, :], scale=1.0 / E_SCALE,
                                             accum_out=chunk_sum[:, par, c:c + 1]).then_inc(exp_made, 1)

            steps(act, step)

            def group(G, slot):
                for t in range(GT):
                    act.wait_ge(z_done, G * GT + t + 1)
                    nc.scalar.activation(out_grp[:, slot, t], banks[:, slot * GT + t, :], ACT.Relu,
                                         scale=1.0 / Y_SCALE).then_inc(relu_made, 1)

            group(0, 0)
            group(1, 1)
            with act.Fori(1, GROUPS // 2) as s:
                for slot in range(2):
                    act.wait_ge(out_stored[slot], s * GT * 16)
                    group(s * 2 + slot, slot)

        @block.vector
        def _(dve):
            def lo_of(to, src, scale, hi, made):
                nc.vector.scalar_tensor_tensor(out=to, in0=src, scalar=scale, in1=hi,
                                               op0=ALU.mult, op1=ALU.subtract).then_inc(made, 1)

            def newton_step(n, width):
                nc.vector.tensor_tensor(newton[:, 0:width], rough[:, 0:width], rough[:, 0:width], ALU.mult).then_inc(stats_made, 1)
                dve.wait_ge(stats_made, n + 1)
                nc.vector.tensor_tensor(newton[:, 0:width], newton[:, 0:width], var_eps[:, 0:width], ALU.mult).then_inc(stats_made, 1)
                dve.wait_ge(stats_made, n + 2)
                nc.vector.tensor_scalar(newton[:, 0:width], newton[:, 0:width], -0.5 * H_SCALE, 1.5 * H_SCALE,
                                        ALU.mult, ALU.add).then_inc(stats_made, 1)
                dve.wait_ge(stats_made, n + 3)
                nc.vector.tensor_tensor(rstd[:, 0:width], newton[:, 0:width], rough[:, 0:width], ALU.mult).then_inc(stats_made, 1)
                dve.wait_ge(stats_made, n + 4)

            GROUP_STATS = GT + 1 + 4

            def gather_stats(g, slot):
                for t in range(GT):
                    nc.vector.bn_stats(stats[:, t, :], xg[:, slot, t]).then_inc(stats_made, 1)

            def normalise(g, slot):
                base = g * GROUP_STATS
                for t in range(GT):
                    last = nc.vector.bn_aggr(moments[:, t, :], stats[:, t, :])
                last.then_inc(stats_made, 1)
                dve.wait_ge(stats_made, base + GT + 1)
                nc.vector.tensor_scalar(var_eps[:, :], moments[:, :, 1], EPS, None, ALU.add).then_inc(var_made, 1)
                dve.wait_ge(rough_made, g + 1)
                newton_step(base + GT + 1, GT)
                for t in range(GT):
                    nc.vector.tensor_scalar(hg[:, slot, t], xg[:, slot, t], moments[:, t, 0:1], rstd[:, t:t + 1],
                                            ALU.subtract, ALU.mult).then_inc(h_made, 1)

            def hT_lo(g, k, slot):
                dve.wait_ge(hT_hi_made, g * KD + k + 1)
                nc.vector.scalar_tensor_tensor(out=hT[:, slot, 1, k], in0=hT_ps[k % 2], scalar=0.0, in1=hT[:, slot, 0, k],
                                               op0=ALU.max, op1=ALU.subtract).then_inc(hT_lo_made, 1)

            def project(g, slot, ahead, x_count):
                for m in range(KD):
                    if ahead:
                        hT_lo(g + 1, m, 1 - slot)
                    dve.wait_ge(g_hi_made, g * KD + m + 1)
                    cols = bass.ds(g * CW, CW)
                    lo_of(gT_lo[:, m, cols], g_ps[m % 2], G_SCALE / (H_SCALE * W_SCALE), gT_hi[:, m, cols], g_lo_made)
                if x_count is not None:
                    dve.wait_ge(xg_in[slot], x_count)
                    dve.wait_ge(hT_done, g * KD + KD)
                    gather_stats(g + 2, slot)
                for t in range(GT):
                    if t == 0 and x_count is not None:
                        dve.wait_ge(stats_made, (g + 2) * GROUP_STATS + GT)
                    dve.wait_ge(s_hi_made, g * GT + t + 1)
                    tile = bass.ds(g * GT + t, 1)
                    lo_of(s_lo[:, tile].rearrange("p o d -> p (o d)"), s_ps[t % 2], S_SCALE / (H_SCALE * W_SCALE),
                          s_hi[:, tile].rearrange("p o d -> p (o d)"), s_lo_made)
                    if t == 0 and x_count is not None:
                        normalise(g + 2, slot)
                dve.wait_ge(node_done, g + 1)
                nc.vector.tensor_scalar(logits[:, bass.ds(g * GT, GT)], node_ps[:, 0:GT], 1.0 / (H_SCALE * W_SCALE), None,
                                        ALU.mult).then_inc(logits_made, 1)

            dve.wait_ge(ones_made, 2)
            dve.wait_ge(xg_in[0], 16)
            gather_stats(0, 0)
            dve.wait_ge(stats_made, 0 * GROUP_STATS + GT)
            normalise(0, 0)
            dve.wait_ge(w_hi_made, 1)
            lo_of(edge_hl[:, 1].rearrange("p k n -> p (k n)"), stage_edge, W_SCALE,
                  edge_hl[:, 0].rearrange("p k n -> p (k n)"), w_lo_made)
            for k in range(KD):
                hT_lo(0, k, 0)
            dve.wait_ge(w_hi_made, 3)
            lo_of(w_hl[:, 1].rearrange("p k n -> p (k n)"), stage_w, W_SCALE,
                  w_hl[:, 0].rearrange("p k n -> p (k n)"), w_lo_made)
            lo_of(node_hl[:, 1], node_f[:, :], W_SCALE, node_hl[:, 0], w_lo_made)
            dve.wait_ge(xg_in[1], 16)
            gather_stats(1, 1)
            dve.wait_ge(stats_made, 1 * GROUP_STATS + GT)
            normalise(1, 1)
            dve.wait_ge(w_hi_made, 4)
            lo_of(w1_hl[:, 1].rearrange("p k n -> p (k n)"), stage_w1, W_SCALE,
                  w1_hl[:, 0].rearrange("p k n -> p (k n)"), w_lo_made)
            project(0, 0, True, 32)
            with dve.Fori(0, (GROUPS - 4) // 2) as s:
                project(s * 2 + 1, 1, True, s * 16 + 32)
                project(s * 2 + 2, 0, True, s * 16 + 48)
            project(GROUPS - 3, 1, True, GROUPS // 2 * 16)
            project(GROUPS - 2, 0, True, None)
            project(GROUPS - 1, 1, False, None)

            dve.wait_ge(logits_made, GROUPS)
            nc.vector.tensor_reduce(out=node_col[:, :], in_=logits[:, :], axis=AX.X, op=ALU.max).then_inc(node_step, 1)
            dve.wait_ge(node_step, 1)
            nc.vector.tensor_scalar(node_row[:, :], ones[:, :], node_col[:, :], None, ALU.mult).then_inc(node_step, 1)

            STATS0 = GROUPS * GROUP_STATS
            TILE_STATS = 2 + 4

            def step(i, parity=0):
                scores, products, layer1, par = parts(i, parity)
                first = isinstance(i, int) and i == 0
                for c in range(CHUNKS):
                    if scores:
                        if layer1 and c == 1:
                            dve.wait_ge(stats_made, STATS0 + (i - 2) * TILE_STATS + 1)
                        if c % 4 == 0:
                            dve.wait_ge(adj_in[par][c // 4], (i - par) * 8 + 16)
                        nc.vector.tensor_scalar(penalty[:, c % 2], adj_sb[:, par, c * CW:(c + 1) * CW], 0.0,
                                                NEG_BIG * E_SCALE, ALU.is_le, ALU.mult).then_inc(penalty_made, 1)
                        if layer1 and c == 1:
                            nc.vector.bn_aggr(moments[:, 0, :], stats[:, 0, :]).then_inc(stats_made, 1)
                        dve.wait_ge(score_done, i * CHUNKS + c + 1)
                        dve.wait_ge(penalty_made, i * CHUNKS + c + 1)
                    if products:
                        dve.wait_ge(pT_hi_made, (i - 1) * CHUNKS + c + 1)
                        lo_of(pT_lo[:, c % 4].rearrange("p b n -> p (b n)"), pT_ps[c % 2], P_SCALE,
                              pT_hi[:, c % 4].rearrange("p b n -> p (b n)"), pT_lo_made)
                    if scores:
                        nc.vector.tensor_tensor_reduce(probs[:, c * CW:(c + 1) * CW], score_ps[c % 2], penalty[:, c % 2],
                                                       1.0, -3.0e38, ALU.add, ALU.max,
                                                       chunk_max[:, c:c + 1]).then_inc(masked, 1)
                    if layer1 and c == 0:
                        dve.wait_ge(x1_made, i - 1)
                        nc.vector.bn_stats(stats[:, 0, :], x1_sb[:, :]).then_inc(stats_made, 1)
                    if layer1 and not scores and c == 1:
                        dve.wait_ge(stats_made, STATS0 + (i - 2) * TILE_STATS + 1)
                        nc.vector.bn_aggr(moments[:, 0, :], stats[:, 0, :]).then_inc(stats_made, 1)
                    if layer1 and c == 1:
                        base = STATS0 + (i - 2) * TILE_STATS
                        dve.wait_ge(stats_made, base + 2)
                        nc.vector.tensor_scalar(var_eps[:, 0:1], moments[:, 0, 1:2], EPS, None, ALU.add).then_inc(var_made, 1)
                        dve.wait_ge(rough_made, i - 1 + GROUPS)
                        newton_step(base + 2, 1)
                        wait_from(dve, h1T_done, i - 2)
                        nc.vector.tensor_scalar(h1_sb[:, :], x1_sb[:, :], moments[:, 0, 0:1], rstd[:, 0:1],
                                                ALU.subtract, ALU.mult).then_inc(h1_made, 1)
                    if layer1 and c == 3:
                        dve.wait_ge(h1T_hi_made, i - 1)
                        nc.vector.scalar_tensor_tensor(out=h1T[:, 1].rearrange("p k n -> p (k n)"), in0=h1T_ps, scalar=0.0,
                                                       in1=h1T[:, 0].rearrange("p k n -> p (k n)"),
                                                       op0=ALU.max, op1=ALU.subtract).then_inc(h1T_lo_made, 1)
                    if layer1 and c == 6:
                        dve.wait_ge(y_hi_made, i - 1)
                        lo_of(y_out[:, 1], y_ps, Y_SCALE / (H_SCALE * W_SCALE), y_out[:, 0], y_lo_made)
                    if first and c == 2:
                        dve.wait_ge(node_row_done, 1)
                        nc.vector.tensor_reduce(out=node_neg[:, :], in_=y_ps[:, 0:P], axis=AX.X, op=ALU.max,
                                                negate=True).then_inc(node_step, 1)
                    if first and c == 6:
                        dve.wait_ge(node_total_done, 1)
                        nc.vector.reciprocal(node_rec[:, :], y_ps[:, 0:1]).then_inc(node_step, 1)
                        dve.wait_ge(node_step, 4)
                        nc.vector.tensor_scalar(node_att[:, :], node_att[:, :], node_rec[:, :], 1.0 / (P_SCALE * S_SCALE),
                                                ALU.mult, ALU.mult).then_inc(node_step, 1)
                if scores:
                    dve.wait_ge(masked, i * CHUNKS + CHUNKS)
                    nc.vector.tensor_reduce(out=row_max[:, :], in_=chunk_max[:, :], axis=AX.X, op=ALU.max).then_inc(max_step, 1)
                    dve.wait_ge(max_step, i * 2 + 1)
                    nc.vector.tensor_scalar(neg_max[:, :], row_max[:, :], -1.0 / E_SCALE, None, ALU.mult).then_inc(max_step, 1)
                    for c in range(CHUNKS):
                        row = probs[:, c * CW:(c + 1) * CW]
                        dve.wait_ge(exp_made, i * CHUNKS + c + 1)
                        nc.vector.tensor_tensor(row, row, adj_sb[:, par, c * CW:(c + 1) * CW], ALU.mult).then_inc(probs_made, 1)
                if products:
                    base = (i - 1) * 3
                    if isinstance(i, int) and i == 1:
                        dve.wait_ge(node_step, 5)
                    nc.vector.reduce_sum(out=row_sum[:, :], in_=chunk_sum[:, 1 - par, :], axis=AX.X).then_inc(sum_step, 1)
                    dve.wait_ge(sum_step, base + 1)
                    nc.vector.reciprocal(row_rec[:, :], row_sum[:, :]).then_inc(sum_step, 1)
                    dve.wait_ge(sum_step, base + 2)
                    nc.vector.tensor_tensor(row_fac[:, :], row_rec[:, :], node_att[:, bass.ds(i - 1, 1)], ALU.mult).then_inc(sum_step, 1)
                    dve.wait_ge(sum_step, base + 3)
                    dve.wait_ge(xb_made, i)
                    wait_from(dve, x1_out, (i - 1) * 16)
                    dve.wait_ge(att_done, i * CHUNKS)
                    nc.vector.scalar_tensor_tensor(out=x1_sb[:, :], in0=att_ps, scalar=row_fac[:, :], in1=x_sb[:, :],
                                                   op0=ALU.mult, op1=ALU.add).then_inc(x1_made, 1)

            steps(dve, step)

            with dve.Fori(0, GROUPS // 2) as s:
                for slot in range(2):
                    dve.wait_ge(x1_in[slot], s * 16 + 16)
                    for t in range(GT):
                        dve.wait_ge(relu_made, (s * 2 + slot) * GT + t + 1)
                        nc.vector.tensor_tensor(out_grp[:, slot, t], out_grp[:, slot, t], x1_grp[:, slot, t],
                                                ALU.add).then_inc(out_made, 1)

        @block.tensor
        def _(pe):
            def product(bank, stationary, moving, done):
                for k in range(KD):
                    for n, (a, b) in enumerate(((0, 0), (0, 1), (1, 0))):
                        last = nc.tensor.matmul(bank, stationary(a, k), moving(b, k), start=(k == 0 and n == 0),
                                                stop=(k == KD - 1 and n == 2))
                last.then_inc(done, 1)

            def transposed(bank, block_of, done):
                for b in range(BPC):
                    last = nc.tensor.transpose(bank[:, b * P:(b + 1) * P], block_of(b), ident[:, :])
                last.then_inc(done, 1)

            def transpose_h(g, k, slot):
                pe.wait_ge(h_made, g * GT + GT)
                wait_from(pe, hT_lo_made, g * KD + k - 1)
                transposed(hT_ps[k % 2], lambda t: hg[:, slot, t, k * P:(k + 1) * P], hT_done)

            def project(g, slot, ahead):
                for m in range(KD):
                    if ahead:
                        transpose_h(g + 1, m, 1 - slot)
                    if m == 0:
                        pe.wait_ge(hT_lo_made, g * KD + KD)
                    wait_from(pe, g_lo_made, g * KD + m - 1)
                    product(g_ps[m % 2], lambda a, k: edge_hl[:, a, k, m * P:(m + 1) * P],
                            lambda b, k: hT[:, slot, b, k, :], g_done)
                if isinstance(g, int) and g == 0:
                    pe.wait_ge(w_lo_made, 3)
                wait_from(pe, logits_made, g)
                for t in range(GT):
                    wait_from(pe, s_lo_made, g * GT + t - 1)
                    rows = slice(t * P, (t + 1) * P)
                    product(s_ps[t % 2], lambda a, k: hT[:, slot, a, k, rows], lambda b, k: w_hl[:, b, k, :], s_done)
                    for k in range(KD):
                        for n, (a, b) in enumerate(((0, 0), (0, 1), (1, 0))):
                            last = nc.tensor.matmul(node_ps[:, t:t + 1], hT[:, slot, a, k, rows], node_hl[:, b, k:k + 1],
                                                    start=(k == 0 and n == 0), stop=(k == KD - 1 and n == 2))
                last.then_inc(node_done, 1)

            pe.wait_ge(ident_made, 2)
            for k in range(KD):
                transpose_h(0, k, 0)
            pe.wait_ge(w_lo_made, 1)
            project(0, 0, True)
            with pe.Fori(0, (GROUPS - 2) // 2) as s:
                project(s * 2 + 1, 1, True)
                project(s * 2 + 2, 0, True)
            project(GROUPS - 1, 1, False)

            def add_products(i, c):
                n = (i - 1) * CHUNKS + c
                pe.wait_ge(pT_lo_made, n + 1)
                if c == 0:
                    wait_from(pe, x1_made, i - 1)
                for b in range(BPC):
                    j = c * BPC + b
                    for m, (pT, s) in enumerate(((pT_hi, s_hi), (pT_hi, s_lo), (pT_lo, s_hi))):
                        last = nc.tensor.matmul(att_ps, pT[:, c % 4, b, :], s[:, j, :], start=(j == 0 and m == 0),
                                                stop=(j == TILES - 1 and m == 2))
                last.then_inc(att_done, 1)

            def step(i, parity=0):
                scores, products, layer1, par = parts(i, parity)
                first = isinstance(i, int) and i == 0
                for c in range(CHUNKS):
                    if products:
                        n = (i - 1) * CHUNKS + c
                        pe.wait_ge(probs_made, n + 1)
                        wait_from(pe, pT_lo_made, n - 1)
                        transposed(pT_ps[c % 2], lambda b: probs[:, c * CW + b * P:c * CW + (b + 1) * P], pT_done)
                    if scores:
                        n = i * CHUNKS + c
                        if c == 0:
                            pe.wait_ge(g_cur_made, i * 2 + 2)
                        wait_from(pe, masked, n - 1)
                        product(score_ps[c % 2], lambda a, k: g_cur[:, a, k, :],
                                lambda b, k: (gT_hi, gT_lo)[b][:, k, c * CW:(c + 1) * CW], score_done)
                        if c % 4 == 0:
                            pe.wait_ge(adj_in[par][c // 4], (i - par) * 8 + 16)
                        wait_from(pe, adjT_made, n)
                        transposed(adjT_ps, lambda b: adj_sb[:, par, c * CW + b * P:c * CW + (b + 1) * P], adjT_done)
                    if layer1 and c == 2:
                        pe.wait_ge(h1_made, i - 1)
                        wait_from(pe, h1T_lo_made, i - 2)
                        transposed(h1T_ps, lambda k: h1_sb[:, k * P:(k + 1) * P], h1T_done)
                    if layer1 and c == 5:
                        pe.wait_ge(h1T_lo_made, i - 1)
                        wait_from(pe, y_lo_made, i - 2)
                        product(y_ps, lambda a, k: h1T[:, a, k, :], lambda b, k: w1_hl[:, b, k, :], y_done)
                    if first and c == 0:
                        pe.wait_ge(node_step, 2)
                        nc.tensor.matmul(y_ps[:, 0:P], node_row[:, :], ident[:, :], start=True, stop=True).then_inc(node_row_done, 1)
                    if first and c == 5:
                        pe.wait_ge(node_exp_made, 1)
                        nc.tensor.matmul(y_ps[:, 0:1], ones[:, :], node_sum[:, :], start=True, stop=True).then_inc(node_total_done, 1)
                    if products and c >= 2:
                        add_products(i, c - 2)
                if products:
                    add_products(i, CHUNKS - 2)
                    add_products(i, CHUNKS - 1)

            pe.wait_ge(s_lo_made, TILES)
            steps(pe, step)

            def group(G, slot, first=False):
                for j in range(TILES):
                    if first:
                        for n, (a, b) in enumerate(Y_LOADS):
                            if j == a:
                                pe.wait_ge(y_in[n], 32)
                    for t in range(GT):
                        for m, y in enumerate((y_hi, y_lo)):
                            last = nc.tensor.matmul(banks[:, slot * GT + t, :], adjT_grp[slot][:, t, j * P:(j + 1) * P],
                                                    y[:, j, :], start=(j == 0 and m == 0), stop=(j == TILES - 1 and m == 1))
                        if j == TILES - 1:
                            last.then_inc(z_done, 1)

            pe.wait_ge(adjT_in[0], 16)
            group(0, 0, first=True)
            pe.wait_ge(adjT_in[1], 16)
            group(1, 1)
            with pe.Fori(1, GROUPS // 2) as s:
                for slot in range(2):
                    pe.wait_ge(adjT_in[slot], s * 16 + 16)
                    pe.wait_ge(relu_made, (s * 2 + slot - 1) * GT)
                    group(s * 2 + slot, slot)


_INS = ["x", "adj", "L0_gnn_weight", "L0_gnn_bias", "L0_gnn_node_w", "L0_gnn_edge_w", "L1_gnn_weight"]


def kernel(**inputs):
    import concourse.bacc as bacc
    from concourse.bass_utils import run_bass_kernel_spmd

    nc = bacc.Bacc("TRN2", target_bir_lowering=False, num_devices=1, dynamic_dma_scratch_size=1024)
    arrays, args = {}, []
    for name in _INS:
        a = np.ascontiguousarray(inputs[name])
        arrays[f"in_{name}"] = a
        args.append(nc.dram_tensor(f"in_{name}", a.shape, mybir.dt.from_np(a.dtype), kind="ExternalInput").ap())
    out = nc.dram_tensor("out", (N, D), mybir.dt.float32, kind="ExternalOutput").ap()
    build_program(nc, *args, out)
    results = run_bass_kernel_spmd(nc, [arrays], core_ids=[0])
    return results.results[0]["out"]
```

```python
from contextlib import ExitStack

import concourse.bass as bass
from concourse import mybir
import numpy as np

P = 128
N, D = 4096, 512
TILES = N // P
KD = D // P
CW = 512
CHUNKS = N // CW
BPC = CW // P
GT = 4
GROUPS = TILES // GT
EPS = 1e-5
NEG_BIG = -9000000000000000.0

H_SCALE = 64.0
W_SCALE = 64.0
G_SCALE = 8.0
S_SCALE = 16.0
P_SCALE = 256.0
Y_SCALE = 64.0
E_SCALE = G_SCALE * G_SCALE


AHEAD = 2
SUPER = CW // P
SUPERS = TILES // SUPER


class Row:

    def __init__(self, R, s, par):
        self.R, self.s, self.par = R, s, par
        self.tile = s * 2 + (SUPER * R + par)
        self.last = isinstance(s, int) and self.tile == TILES - 1
        computed, moved = CHUNKS - R, CHUNKS - 1 - R
        self.computed0 = s * (2 * computed) + (sum(SUPER * (CHUNKS - r) for r in range(R)) + par * computed)
        self.moved0 = s * (2 * moved) + (sum(SUPER * (CHUNKS - 1 - r) for r in range(R)) + par * moved)
        self.moved_half = s * moved + sum(SUPER // 2 * (CHUNKS - 1 - r) for r in range(R))
        self.loaded_half = s * R + sum(SUPER // 2 * r for r in range(R))

    def score_bank(self, c):
        return (self.par * (CHUNKS - self.R) + c - self.R) % 2

    def moved_slot(self, c):
        return (self.par * (CHUNKS - 1 - self.R) + c - self.R - 1) % 2

    def moved_uses(self, c):
        return self.moved_half + (self.par * (CHUNKS - 1 - self.R) + c - self.R - 1) // 2

    def loaded_slot(self, c):
        return (self.par * self.R + c) % 2

    def loaded_uses(self, c):
        return self.loaded_half + (self.par * self.R + c) // 2


def wait_from(engine, semaphore, value):
    if isinstance(value, int) and value <= 0:
        return
    engine.wait_ge(semaphore, value)


def build_program(nc, x, adj, weight, bias, node_w, edge_w, weight1, out):
    f32, f16 = mybir.dt.float32, mybir.dt.float16
    ALU, ACT, AX = mybir.AluOpType, mybir.ActivationFunctionType, mybir.AxisListType

    adjT_dram = nc.dram_tensor("adjT_scratch", (TILES, P, N), f16, kind="Internal").ap()
    y_dram = nc.dram_tensor("y_scratch", (TILES, P, 2, D), f16, kind="Internal").ap()
    scores_dram = nc.dram_tensor("scores_scratch", (TILES, P, N), f32, kind="Internal").ap()
    x1_dram = nc.dram_tensor("x1_scratch", (TILES, P, D), f32, kind="Internal").ap()

    x_groups = x.rearrange("(g t p) d -> g p t d", t=GT, p=P)
    x_tiles = x.rearrange("(t p) d -> t p d", p=P)
    adj_tiles = adj.rearrange("(t p) n -> t p n", p=P)
    out_tiles = out.rearrange("(t p) d -> t p d", p=P)

    with ExitStack() as ctx:
        def sb(name, shape, dt):
            return ctx.enter_context(nc.sbuf_tensor(name, shape, dt))

        def sem(name):
            return ctx.enter_context(nc.semaphore(name))

        gT_hi = sb("gT_hi", [P, KD, N], f16)
        gT_lo = sb("gT_lo", [P, KD, N], f16)
        s_hi = sb("s_hi", [P, TILES, D], f16)
        s_lo = sb("s_lo", [P, TILES, D], f16)
        probs = sb("probs", [P, N], f32)
        adj_sb = sb("adj_sb", [P, 2, N], f32)
        w1_hl = sb("w1_hl", [P, 2, KD, D], f16)
        shared = sb("shared", [P, 8192], f16)
        g_cur = sb("g_cur", [P, 2, KD, P], f16)
        x_sb = sb("x_sb", [P, D], f32)
        scoresT_sb = sb("scoresT_sb", [P, 2, BPC, P], f32)
        loaded = sb("loaded", [P, 2, CW], f32)
        h1_sb = sb("h1_sb", [P, D], f32)
        h1T = sb("h1T", [P, 2, KD, P], f16)
        y_out = sb("y_out", [P, 2, D], f16)
        bias_sb = sb("bias_sb", [P, D], f32)
        ident = sb("ident", [P, P], f32)
        ident_16 = sb("ident_16", [P, P], f16)
        ones = sb("ones", [P, P], f32)
        half = sb("half", [P, GT], f32)
        node_f = sb("node_f", [P, KD], f32)
        node_hl = sb("node_hl", [P, 2, KD], f16)
        logits = sb("logits", [P, TILES], f32)
        node_att = sb("node_att", [P, TILES], f32)
        node_col = sb("node_col", [P, 1], f32)
        node_neg = sb("node_neg", [P, 1], f32)
        node_sum = sb("node_sum", [P, 1], f32)
        node_rec = sb("node_rec", [P, 1], f32)
        node_row = loaded[:, 0, 0:P]
        stats = sb("stats", [P, GT, 6], f32)
        moments = sb("moments", [P, GT, 2], f32)
        var_eps = sb("var_eps", [P, GT], f32)
        rough = sb("rough", [P, GT], f32)
        newton = sb("newton", [P, GT], f32)
        rstd = sb("rstd", [P, GT], f32)
        chunk_max = sb("chunk_max", [P, CHUNKS], f32)
        row_max = sb("row_max", [P, 1], f32)
        neg_max = sb("neg_max", [P, 1], f32)
        chunk_sum = sb("chunk_sum", [P, 2, CHUNKS], f32)
        row_sum = sb("row_sum", [P, 1], f32)
        row_rec = sb("row_rec", [P, 1], f32)
        row_fac = sb("row_fac", [P, 1], f32)

        edge_hl = shared[:, 0:4096].rearrange("p (h k n) -> p h k n", h=2, k=KD)
        w_hl = shared[:, 4096:8192].rearrange("p (h k n) -> p h k n", h=2, k=KD)
        hT = probs[:, :].bitcast(f16).rearrange("p (s h k n) -> p s h k n", s=2, h=2, k=KD)
        xg = adj_sb[:, 0, :].rearrange("p (s t d) -> p s t d", s=2, t=GT)
        hg = adj_sb[:, 1, :].rearrange("p (s t d) -> p s t d", s=2, t=GT)
        stage_edge = s_lo[:, 24:32, :].rearrange("p a b -> p (a b)").bitcast(f32)
        stage_w = s_hi[:, 24:32, :].rearrange("p a b -> p (a b)").bitcast(f32)
        stage_w1 = s_hi[:, 16:24, :].rearrange("p a b -> p (a b)").bitcast(f32)
        penalty = shared[:, 0:1024].bitcast(mybir.dt.bfloat16).rearrange("p (s n) -> p s n", s=2)
        adj_16 = shared[:, 1024:2048].rearrange("p (s n) -> p s n", s=2)
        pT_hi = shared[:, 2048:3072].rearrange("p (s b n) -> p s b n", s=2, b=BPC)
        pT_lo = shared[:, 3072:4096].rearrange("p (s b n) -> p s b n", s=2, b=BPC)
        adjT_sb = shared[:, 4096:6144].rearrange("p (s n) -> p s n", s=2)
        raw = shared[:, 6144:8192].bitcast(f32).rearrange("p (s n) -> p s n", s=2)
        y_hi = gT_hi[:, :, :].rearrange("p k n -> p (k n)").rearrange("p (j d) -> p j d", d=D)
        y_lo = gT_lo[:, :, :].rearrange("p k n -> p (k n)").rearrange("p (j d) -> p j d", d=D)
        adjT_grp = [adj_sb[:, :, :].rearrange("p s n -> p (s n)").bitcast(f16).rearrange("p (t n) -> p t n", t=GT),
                    s_hi[:, :, :].rearrange("p j d -> p (j d)").rearrange("p (t n) -> p t n", t=GT)]
        x1_grp = probs[:, :].rearrange("p (s t d) -> p s t d", s=2, t=GT)
        out_grp = s_lo[:, :, :].rearrange("p j d -> p (j d)").bitcast(f32).rearrange(
            "p (s t d) -> p s t d", s=4, t=GT)

        banks = ctx.enter_context(nc.psum_tensor("banks", [P, 8, 512], f32))
        hT_ps = [banks[:, b, :] for b in (0, 1)]
        g_ps = [banks[:, b, :] for b in (2, 3)]
        s_ps = [banks[:, b, :] for b in (4, 5)]
        node_ps = banks[:, 6, :]
        score_ps = [banks[:, b, :] for b in (0, 1)]
        pT_ps = [banks[:, b, :] for b in (2, 3)]
        adjT_ps = banks[:, 4, 0:CW // 2].bitcast(f16)
        att_ps = banks[:, 5, :]
        h1T_ps = y_ps = banks[:, 6, :]
        scoresT_ps = banks[:, 7, :]

        ident_made = sem("ident_made")
        ones_made = sem("ones_made")
        edge_in = sem("edge_in")
        weight_in = sem("weight_in")
        w1_in = sem("w1_in")
        node_in = sem("node_in")
        bias_in = sem("bias_in")
        w_hi_made = sem("w_hi_made")
        w_lo_made = sem("w_lo_made")
        xg_in = [sem("xg_in0"), sem("xg_in1")]
        stats_made = sem("stats_made")
        var_made = sem("var_made")
        rough_made = sem("rough_made")
        h_made = sem("h_made")
        hT_done = sem("hT_done")
        hT_hi_made = sem("hT_hi_made")
        hT_lo_made = sem("hT_lo_made")
        g_done = sem("g_done")
        g_hi_made = sem("g_hi_made")
        g_lo_made = sem("g_lo_made")
        s_done = sem("s_done")
        s_hi_made = sem("s_hi_made")
        s_lo_made = sem("s_lo_made")
        node_done = sem("node_done")
        logits_made = sem("logits_made")
        node_step = sem("node_step")
        node_row_done = sem("node_row_done")
        node_exp_made = sem("node_exp_made")
        node_total_done = sem("node_total_done")
        adj_in = [[sem("adj_in00"), sem("adj_in01")], [sem("adj_in10"), sem("adj_in11")]]
        x_in = sem("x_in")
        xb_made = sem("xb_made")
        g_cur_made = sem("g_cur_made")
        penalty_made = sem("penalty_made")
        score_done = sem("score_done")
        masked = sem("masked")
        raw_made = sem("raw_made")
        scoresT_done = sem("scoresT_done")
        scoresT_made = sem("scoresT_made")
        scoresT_out = [sem("scoresT_out0"), sem("scoresT_out1")]
        loaded_in = [sem("loaded_in0"), sem("loaded_in1")]
        max_step = sem("max_step")
        exp_made = sem("exp_made")
        probs_made = sem("probs_made")
        pT_done = sem("pT_done")
        pT_hi_made = sem("pT_hi_made")
        pT_lo_made = sem("pT_lo_made")
        att_done = sem("att_done")
        adj_16_made = sem("adj_16_made")
        adjT_done = sem("adjT_done")
        adjT_made = sem("adjT_made")
        adjT_out = [sem("adjT_out0"), sem("adjT_out1")]
        sum_step = sem("sum_step")
        x1_made = sem("x1_made")
        x1_out = sem("x1_out")
        h1_made = sem("h1_made")
        h1T_done = sem("h1T_done")
        h1T_hi_made = sem("h1T_hi_made")
        h1T_lo_made = sem("h1T_lo_made")
        y_done = sem("y_done")
        y_hi_made = sem("y_hi_made")
        y_lo_made = sem("y_lo_made")
        y_stored = sem("y_stored")
        Y_LOADS = [(0, 16), (16, 28), (28, 31), (31, 32)]
        y_in = [sem(f"y_in{n}") for n in range(len(Y_LOADS))]
        adjT_in = [sem("adjT_in0"), sem("adjT_in1")]
        x1_in = [sem("x1_in0"), sem("x1_in1")]
        z_done = sem("z_done")
        relu_made = sem("relu_made")
        out_made = sem("out_made")
        out_stored = [sem("out_stored0"), sem("out_stored1")]

        block = ctx.enter_context(nc.Block())

        def steps(engine, step, unroll_last=False):
            for par in range(2):
                step(par, Row(0, 0, par))
            for par in range(2):
                step(2 + par, Row(0, 1, par))
            for R in range(1, SUPERS):
                if unroll_last and R == SUPERS - 1:
                    for s in range(SUPER // 2):
                        for par in range(2):
                            row = Row(R, s, par)
                            step(row.tile, row)
                else:
                    with engine.Fori(0, SUPER // 2) as s:
                        for par in range(2):
                            row = Row(R, s, par)
                            step(row.tile, row)

        def parts(i, row):
            if isinstance(i, int):
                return row is not None, 1 <= i <= TILES, i >= 2
            return True, True, True

        @block.sync
        def _(sp):
            sp.dma_start(xg[:, 0], x_groups[0]).then_inc(xg_in[0], 16)
            sp.dma_start(stage_edge.rearrange("p (k n) -> p k n", k=KD),
                         edge_w.rearrange("(k p) n -> p k n", p=P)).then_inc(edge_in, 16)
            sp.dma_start(xg[:, 1], x_groups[1]).then_inc(xg_in[1], 16)
            sp.dma_start(stage_w.rearrange("p (k n) -> p k n", k=KD),
                         weight.rearrange("(k p) n -> p k n", p=P)).then_inc(weight_in, 16)
            with nc.allow_non_contiguous_dma(reason="512 words, once"):
                sp.dma_start(node_f[:, :], node_w.rearrange("(k p) o -> p (k o)", p=P)).then_inc(node_in, 16)
            sp.dma_start(stage_w1.rearrange("p (k n) -> p k n", k=KD),
                         weight1.rearrange("(k p) n -> p k n", p=P)).then_inc(w1_in, 16)
            sp.dma_start(bias_sb[:, :], bias.rearrange("(o n) -> o n", o=1).to_broadcast((P, D))).then_inc(bias_in, 16)
            with sp.Fori(0, (GROUPS - 2) // 2) as s:
                for half_ in range(2):
                    g = s * 2 + half_
                    sp.wait_ge(h_made, g * GT + GT)
                    sp.dma_start(xg[:, half_], x_groups[bass.ds(g + 2, 1)].rearrange("o p t d -> (o p) t d")
                                 ).then_inc(xg_in[half_], 16)

            def load_adj(i, slot, hf):
                cols = slice(hf * N // 2, (hf + 1) * N // 2)
                sp.dma_start(adj_sb[:, slot, cols], adj_tiles[bass.ds(i, 1), :, cols].rearrange("o p n -> (o p) n")
                             ).then_inc(adj_in[slot][hf], 16)

            def load_x(i):
                sp.dma_start(x_sb[:, :], x_tiles[bass.ds(i, 1)].rearrange("o p d -> (o p) d")).then_inc(x_in, 16)

            sp.wait_ge(h_made, TILES)
            load_adj(0, 0, 0)
            load_adj(0, 0, 1)
            load_x(0)

            def load_scores(row, c):
                i = row.tile
                sp.wait_ge(masked, i * CHUNKS + (c - 1 if c >= 2 else 0))
                sp.dma_start(loaded[:, row.loaded_slot(c), :],
                             scores_dram[bass.ds(i, 1), :, c * CW:(c + 1) * CW].rearrange("o p n -> (o p) n")
                             ).then_inc(loaded_in[row.loaded_slot(c)], 16)

            def store_scoresT(row, c):
                slot = row.moved_slot(c)
                sp.wait_ge(scoresT_made, row.moved0 + c - row.R)
                sp.dma_start(scores_dram[c * BPC:(c + 1) * BPC, :, bass.ds(row.tile * P, P)].rearrange("b p n -> p b n"),
                             scoresT_sb[:, slot]).then_inc(scoresT_out[slot], 16)

            def store_y(y):
                sp.wait_ge(y_lo_made, y + 1)
                sp.dma_start(y_dram[bass.ds(y, 1)].rearrange("o p h d -> (o p) h d"), y_out[:, :, :]).then_inc(y_stored, 16)

            def step(i, row=None):
                scores, products, layer1 = parts(i, row)
                R = row.R if row else 0
                if scores and R:
                    for sl in range(2):
                        sp.wait_ge(scoresT_out[sl], 16 * sum(SUPER // 2 * (CHUNKS - 1 - r) for r in range(R)))
                    for c in range(min(R, 2)):
                        load_scores(row, c)
                if layer1:
                    sp.wait_ge(x1_made, i - 1)
                    sp.dma_start(x1_dram[bass.ds(i - 2, 1)].rearrange("o p d -> (o p) d"), x_sb[:, :]).then_inc(x1_out, 16)
                if scores and not products:
                    sp.wait_ge(hT_done, GROUPS * KD)
                    load_adj(1, 1, 0)
                    load_adj(1, 1, 1)
                for c in range(2, CHUNKS):
                    if scores and products and not row.last and c in (4, 7):
                        sp.wait_ge(probs_made, i * CHUNKS - (4 if c == 4 else 0))
                        load_adj(i + 1, 1 - row.par, 0 if c == 4 else 1)
                    if scores and c < R:
                        load_scores(row, c)
                    if scores and c > R + 1:
                        store_scoresT(row, c - 1)
                    if layer1 and products and c == 5:
                        sp.wait_ge(x1_out, (i - 1) * 16)
                        sp.wait_ge(h1_made, i - 1)
                        load_x(i - 1)
                if scores and R < CHUNKS - 1:
                    store_scoresT(row, CHUNKS - 1)
                if layer1:
                    store_y(i - 2)

            steps(sp, step, unroll_last=True)

            def load_y(n):
                a, b = Y_LOADS[n]
                for hl, to in ((0, y_hi), (1, y_lo)):
                    sp.dma_start(to[:, a:b, :], y_dram[a:b, :, hl, :].rearrange("j p d -> p j d")).then_inc(y_in[n], 16)

            def load_adjT(G, slot):
                sp.dma_start(adjT_grp[slot], adjT_dram[bass.ds(G * GT, GT)].rearrange("t p n -> p t n")).then_inc(adjT_in[slot], 16)

            def load_x1(G, slot):
                sp.dma_start(x1_grp[:, slot], x1_dram[bass.ds(G * GT, GT)].rearrange("t p d -> p t d")).then_inc(x1_in[slot], 16)

            sp.wait_ge(score_done, SUPER * sum(CHUNKS - R for R in range(SUPERS)))
            sp.wait_ge(y_stored, 28 * 16)
            load_y(0)
            load_y(1)
            sp.wait_ge(probs_made, TILES * CHUNKS)
            for sl in range(2):
                sp.wait_ge(adjT_out[sl], TILES * 2 * 16)
            load_adjT(0, 0)
            step(TILES)
            sp.wait_ge(y_stored, 31 * 16)
            load_y(2)
            sp.wait_ge(pT_done, TILES * CHUNKS)
            sp.wait_ge(x1_out, 31 * 16)
            load_x1(0, 0)
            load_x1(1, 1)
            sp.wait_ge(att_done, TILES * CHUNKS)
            load_adjT(1, 1)
            step(TILES + 1)
            sp.wait_ge(y_stored, TILES * 16)
            load_y(3)
            sp.wait_ge(x1_out, TILES * 16)

            def group(G, slot, ahead):
                if ahead:
                    sp.wait_ge(z_done, G * GT + GT)
                    load_adjT(G + 2, slot)
                for t in range(GT):
                    sp.wait_ge(out_made, G * GT + t + 1)
                    sp.dma_start(out_tiles[bass.ds(G * GT + t, 1)].rearrange("o p d -> (o p) d"),
                                 out_grp[:, slot, t]).then_inc(out_stored[slot], 16)
                if ahead:
                    load_x1(G + 2, slot)

            with sp.Fori(0, GROUPS // 2 - 1) as s:
                group(s * 2, 0, True)
                group(s * 2 + 1, 1, True)
            group(GROUPS - 2, 0, False)
            group(GROUPS - 1, 1, False)
            for sl in range(2):
                sp.wait_ge(out_stored[sl], GROUPS // 2 * GT * 16)

        @block.gpsimd
        def _(pool):
            nc.gpsimd.memset(ident[:, :], 0.0).then_inc(ident_made, 1)
            pool.wait_ge(ident_made, 1)
            nc.gpsimd.affine_select(out=ident[:, :], in_=ident[:, :], compare_op=ALU.not_equal, fill=1.0,
                                    base=0, pattern=[[-1, P]], channel_multiplier=1).then_inc(ident_made, 1)
            pool.wait_ge(ident_made, 2)
            nc.gpsimd.tensor_copy(ident_16[:, :], ident[:, :]).then_inc(ident_made, 1)
            nc.gpsimd.memset(half[:, :], -0.5).then_inc(ones_made, 1)
            nc.gpsimd.memset(ones[:, :], 1.0).then_inc(ones_made, 1)
            pool.wait_ge(ones_made, 2)
            with pool.Fori(0, GROUPS) as g:
                pool.wait_ge(var_made, g + 1)
                nc.gpsimd.tensor_tensor(rough[:, :], var_eps[:, :], half[:, :], ALU.pow).then_inc(rough_made, 1)
            pool.wait_ge(bias_in, 16)

            def copy_g(i):
                for hl, src in ((0, gT_hi), (1, gT_lo)):
                    nc.gpsimd.tensor_copy(g_cur[:, hl], src[:, :, bass.ds(i * P, P)]).then_inc(g_cur_made, 1)

            pool.wait_ge(g_lo_made, GROUPS * KD)
            pool.wait_ge(g_hi_made, GROUPS * KD)
            copy_g(0)

            def cast_adj(i, par, chunks):
                for c in chunks:
                    if c % 4 == 0:
                        pool.wait_ge(adj_in[par][c // 4], (i - par) * 8 + 16)
                    wait_from(pool, adjT_done, i * CHUNKS + c - 1)
                    nc.gpsimd.tensor_tensor(adj_16[:, c % 2], adj_sb[:, par, c * CW:(c + 1) * CW],
                                            ones[:, 0:1].to_broadcast((P, CW)), ALU.mult).then_inc(adj_16_made, 1)

            pool.wait_ge(node_done, GROUPS)
            cast_adj(0, 0, [0])

            def step(i, row=None):
                scores, products, layer1 = parts(i, row)
                par = row.par if row else 0
                if scores:
                    cast_adj(i, par, range(1, 4))
                if layer1:
                    pool.wait_ge(var_made, i - 1 + GROUPS)
                    nc.gpsimd.tensor_tensor(rough[:, 0:1], var_eps[:, 0:1], half[:, 0:1], ALU.pow).then_inc(rough_made, 1)
                if scores:
                    cast_adj(i, par, range(4, CHUNKS))
                if products:
                    pool.wait_ge(x_in, i * 16)
                    nc.gpsimd.tensor_tensor(x_sb[:, :], x_sb[:, :], bias_sb[:, :], ALU.add).then_inc(xb_made, 1)
                if scores and not row.last:
                    cast_adj(i + 1, 1 - par, [0])
                    pool.wait_ge(score_done, row.computed0 + CHUNKS - row.R)
                    copy_g(i + 1)

            steps(pool, step, unroll_last=True)
            step(TILES)
            step(TILES + 1)

        @block.scalar
        def _(act):
            def hi_of_weight(to, src, arrived):
                act.wait_ge(arrived, 16)
                nc.scalar.activation(to, src, ACT.Copy, scale=W_SCALE).then_inc(w_hi_made, 1)

            hi_of_weight(edge_hl[:, 0].rearrange("p k n -> p (k n)"), stage_edge, edge_in)
            hi_of_weight(w_hl[:, 0].rearrange("p k n -> p (k n)"), stage_w, weight_in)
            hi_of_weight(node_hl[:, 0], node_f[:, :], node_in)

            def hT_hi(g, k, slot):
                act.wait_ge(hT_done, g * KD + k + 1)
                wait_from(act, node_done, g - 1)
                nc.scalar.activation(hT[:, slot, 0, k], hT_ps[k % 2], ACT.Relu).then_inc(hT_hi_made, 1)

            def project(g, slot, ahead):
                for m in range(KD):
                    if ahead:
                        hT_hi(g + 1, m, 1 - slot)
                    act.wait_ge(g_done, g * KD + m + 1)
                    nc.scalar.activation(gT_hi[:, m, bass.ds(g * CW, CW)], g_ps[m % 2], ACT.Copy,
                                         scale=G_SCALE / (H_SCALE * W_SCALE)).then_inc(g_hi_made, 1)
                for t in range(GT):
                    act.wait_ge(s_done, g * GT + t + 1)
                    nc.scalar.activation(s_hi[:, bass.ds(g * GT + t, 1)].rearrange("p o d -> p (o d)"), s_ps[t % 2],
                                         ACT.Copy, scale=S_SCALE / (H_SCALE * W_SCALE)).then_inc(s_hi_made, 1)

            for k in range(KD):
                hT_hi(0, k, 0)
            hi_of_weight(w1_hl[:, 0].rearrange("p k n -> p (k n)"), stage_w1, w1_in)
            project(0, 0, True)
            with act.Fori(0, (GROUPS - 2) // 2) as s:
                project(s * 2 + 1, 1, True)
                project(s * 2 + 2, 0, True)
            project(GROUPS - 1, 1, False)

            def exp_chunk(c, par):
                piece = probs[:, c * CW:(c + 1) * CW]
                nc.scalar.activation(piece, piece, ACT.Exp, bias=neg_max[:, :], scale=1.0 / E_SCALE,
                                     accum_out=chunk_sum[:, par, c:c + 1]).then_inc(exp_made, 1)

            def copy_scoresT(row, c):
                act.wait_ge(scoresT_done, row.moved0 + c - row.R)
                slot = row.moved_slot(c)
                wait_from(act, scoresT_out[slot], row.moved_uses(c) * 16)
                nc.scalar.activation(scoresT_sb[:, slot].rearrange("p b n -> p (b n)"), scoresT_ps,
                                     ACT.Copy).then_inc(scoresT_made, 1)

            def store_adjT(i, pair):
                act.wait_ge(adjT_made, i * CHUNKS + 2 * pair + 2)
                act.dma_start(adjT_dram[bass.ds(i, 1), :, pair * 1024:(pair + 1) * 1024].rearrange("o p n -> (o p) n"),
                              adjT_sb[:, pair % 2, :]).then_inc(adjT_out[pair % 2], 16)

            def step(i, row=None):
                scores, products, layer1 = parts(i, row)
                par = row.par if row else 0
                first = isinstance(i, int) and i == 0
                for c in range(CHUNKS):
                    if scores and c in (2, 4, 6):
                        store_adjT(i, c // 2 - 1)
                    if products:
                        n = (i - 1) * CHUNKS + c
                        act.wait_ge(pT_done, n + 1)
                        wait_from(act, att_done, n - 1)
                        nc.scalar.activation(pT_hi[:, c % 2].rearrange("p b n -> p (b n)"), pT_ps[c % 2], ACT.Copy,
                                             scale=P_SCALE).then_inc(pT_hi_made, 1)
                        if c + AHEAD < CHUNKS:
                            exp_chunk(c + AHEAD, 1 - par)
                    if scores and c > row.R:
                        act.wait_ge(masked, i * CHUNKS + c + 1)
                        wait_from(act, scoresT_done, row.moved0 + c - row.R - 2)
                        nc.scalar.activation(raw[:, row.moved_slot(c), :], score_ps[row.score_bank(c)],
                                             ACT.Copy).then_inc(raw_made, 1)
                    if scores and c > row.R + 1:
                        copy_scoresT(row, c - 1)
                    if scores:
                        act.wait_ge(adjT_done, i * CHUNKS + c + 1)
                        if c % 2 == 0:
                            wait_from(act, adjT_out[(c // 2) % 2], (i * 2 + c // 4) * 16)
                        nc.scalar.activation(adjT_sb[:, (c // 2) % 2, (c % 2) * CW:(c % 2 + 1) * CW], adjT_ps,
                                             ACT.Copy).then_inc(adjT_made, 1)
                    if layer1 and c == 6:
                        act.wait_ge(h1T_done, i - 1)
                        nc.scalar.activation(h1T[:, 0].rearrange("p k n -> p (k n)"), h1T_ps, ACT.Relu).then_inc(h1T_hi_made, 1)
                    if first and c == 4:
                        act.wait_ge(node_step, 3)
                        nc.scalar.activation(node_att[:, :], logits[:, :], ACT.Exp, bias=node_neg[:, :],
                                             accum_out=node_sum[:, :]).then_inc(node_exp_made, 1)
                if scores:
                    store_adjT(i, CHUNKS // 2 - 1)
                    act.wait_ge(max_step, i * 2 + 2)
                    for c in range(AHEAD):
                        exp_chunk(c, par)
                    if row.R < CHUNKS - 1:
                        copy_scoresT(row, CHUNKS - 1)
                if layer1:
                    act.wait_ge(y_done, i - 1)
                    wait_from(act, y_stored, (i - 2) * 16)
                    nc.scalar.activation(y_out[:, 0], y_ps, ACT.Copy,
                                         scale=Y_SCALE / (H_SCALE * W_SCALE)).then_inc(y_hi_made, 1)

            steps(act, step)
            step(TILES)
            step(TILES + 1)

            def group(G, slot):
                for t in range(GT):
                    act.wait_ge(z_done, G * GT + t + 1)
                    nc.scalar.activation(out_grp[:, slot, t], banks[:, slot * GT + t, :], ACT.Relu,
                                         scale=1.0 / Y_SCALE).then_inc(relu_made, 1)

            group(0, 0)
            group(1, 1)
            with act.Fori(1, GROUPS // 2) as s:
                for slot in range(2):
                    act.wait_ge(out_stored[slot], s * GT * 16)
                    group(s * 2 + slot, slot)

        @block.vector
        def _(dve):
            def lo_of(to, src, scale, hi, made):
                nc.vector.scalar_tensor_tensor(out=to, in0=src, scalar=scale, in1=hi,
                                               op0=ALU.mult, op1=ALU.subtract).then_inc(made, 1)

            def newton_step(n, width):
                nc.vector.tensor_tensor(newton[:, 0:width], rough[:, 0:width], rough[:, 0:width], ALU.mult).then_inc(stats_made, 1)
                dve.wait_ge(stats_made, n + 1)
                nc.vector.tensor_tensor(newton[:, 0:width], newton[:, 0:width], var_eps[:, 0:width], ALU.mult).then_inc(stats_made, 1)
                dve.wait_ge(stats_made, n + 2)
                nc.vector.tensor_scalar(newton[:, 0:width], newton[:, 0:width], -0.5 * H_SCALE, 1.5 * H_SCALE,
                                        ALU.mult, ALU.add).then_inc(stats_made, 1)
                dve.wait_ge(stats_made, n + 3)
                nc.vector.tensor_tensor(rstd[:, 0:width], newton[:, 0:width], rough[:, 0:width], ALU.mult).then_inc(stats_made, 1)
                dve.wait_ge(stats_made, n + 4)

            GROUP_STATS = GT + 1 + 4

            def gather_stats(g, slot):
                for t in range(GT):
                    nc.vector.bn_stats(stats[:, t, :], xg[:, slot, t]).then_inc(stats_made, 1)

            def normalise(g, slot):
                base = g * GROUP_STATS
                for t in range(GT):
                    last = nc.vector.bn_aggr(moments[:, t, :], stats[:, t, :])
                last.then_inc(stats_made, 1)
                dve.wait_ge(stats_made, base + GT + 1)
                nc.vector.tensor_scalar(var_eps[:, :], moments[:, :, 1], EPS, None, ALU.add).then_inc(var_made, 1)
                dve.wait_ge(rough_made, g + 1)
                newton_step(base + GT + 1, GT)
                for t in range(GT):
                    nc.vector.tensor_scalar(hg[:, slot, t], xg[:, slot, t], moments[:, t, 0:1], rstd[:, t:t + 1],
                                            ALU.subtract, ALU.mult).then_inc(h_made, 1)

            def hT_lo(g, k, slot):
                dve.wait_ge(hT_hi_made, g * KD + k + 1)
                nc.vector.scalar_tensor_tensor(out=hT[:, slot, 1, k], in0=hT_ps[k % 2], scalar=0.0, in1=hT[:, slot, 0, k],
                                               op0=ALU.max, op1=ALU.subtract).then_inc(hT_lo_made, 1)

            def project(g, slot, ahead, x_count):
                for m in range(KD):
                    if ahead:
                        hT_lo(g + 1, m, 1 - slot)
                    dve.wait_ge(g_hi_made, g * KD + m + 1)
                    cols = bass.ds(g * CW, CW)
                    lo_of(gT_lo[:, m, cols], g_ps[m % 2], G_SCALE / (H_SCALE * W_SCALE), gT_hi[:, m, cols], g_lo_made)
                if x_count is not None:
                    dve.wait_ge(xg_in[slot], x_count)
                    dve.wait_ge(hT_done, g * KD + KD)
                    gather_stats(g + 2, slot)
                for t in range(GT):
                    if t == 0 and x_count is not None:
                        dve.wait_ge(stats_made, (g + 2) * GROUP_STATS + GT)
                    dve.wait_ge(s_hi_made, g * GT + t + 1)
                    tile = bass.ds(g * GT + t, 1)
                    lo_of(s_lo[:, tile].rearrange("p o d -> p (o d)"), s_ps[t % 2], S_SCALE / (H_SCALE * W_SCALE),
                          s_hi[:, tile].rearrange("p o d -> p (o d)"), s_lo_made)
                    if t == 0 and x_count is not None:
                        normalise(g + 2, slot)
                dve.wait_ge(node_done, g + 1)
                nc.vector.tensor_scalar(logits[:, bass.ds(g * GT, GT)], node_ps[:, 0:GT], 1.0 / (H_SCALE * W_SCALE), None,
                                        ALU.mult).then_inc(logits_made, 1)

            dve.wait_ge(ones_made, 2)
            dve.wait_ge(xg_in[0], 16)
            gather_stats(0, 0)
            dve.wait_ge(stats_made, 0 * GROUP_STATS + GT)
            normalise(0, 0)
            dve.wait_ge(w_hi_made, 1)
            lo_of(edge_hl[:, 1].rearrange("p k n -> p (k n)"), stage_edge, W_SCALE,
                  edge_hl[:, 0].rearrange("p k n -> p (k n)"), w_lo_made)
            for k in range(KD):
                hT_lo(0, k, 0)
            dve.wait_ge(w_hi_made, 3)
            lo_of(w_hl[:, 1].rearrange("p k n -> p (k n)"), stage_w, W_SCALE,
                  w_hl[:, 0].rearrange("p k n -> p (k n)"), w_lo_made)
            lo_of(node_hl[:, 1], node_f[:, :], W_SCALE, node_hl[:, 0], w_lo_made)
            dve.wait_ge(xg_in[1], 16)
            gather_stats(1, 1)
            dve.wait_ge(stats_made, 1 * GROUP_STATS + GT)
            normalise(1, 1)
            dve.wait_ge(w_hi_made, 4)
            lo_of(w1_hl[:, 1].rearrange("p k n -> p (k n)"), stage_w1, W_SCALE,
                  w1_hl[:, 0].rearrange("p k n -> p (k n)"), w_lo_made)
            project(0, 0, True, 32)
            with dve.Fori(0, (GROUPS - 4) // 2) as s:
                project(s * 2 + 1, 1, True, s * 16 + 32)
                project(s * 2 + 2, 0, True, s * 16 + 48)
            project(GROUPS - 3, 1, True, GROUPS // 2 * 16)
            project(GROUPS - 2, 0, True, None)
            project(GROUPS - 1, 1, False, None)

            dve.wait_ge(logits_made, GROUPS)
            nc.vector.tensor_reduce(out=node_col[:, :], in_=logits[:, :], axis=AX.X, op=ALU.max).then_inc(node_step, 1)
            dve.wait_ge(node_step, 1)
            nc.vector.tensor_scalar(node_row[:, :], ones[:, :], node_col[:, :], None, ALU.mult).then_inc(node_step, 1)

            def make_penalty(i, c, par):
                if c % 4 == 0:
                    dve.wait_ge(adj_in[par][c // 4], (i - par) * 8 + 16)
                wait_from(dve, masked, i * CHUNKS + c - 1)
                nc.vector.tensor_scalar(penalty[:, c % 2], adj_sb[:, par, c * CW:(c + 1) * CW], 0.0,
                                        NEG_BIG * E_SCALE, ALU.is_le, ALU.mult).then_inc(penalty_made, 1)

            def times_adj(i, c, par):
                dve.wait_ge(exp_made, i * CHUNKS + c + 1)
                piece = probs[:, c * CW:(c + 1) * CW]
                nc.vector.tensor_tensor(piece, piece, adj_sb[:, par, c * CW:(c + 1) * CW], ALU.mult).then_inc(probs_made, 1)

            def wait_for_scores(i, row, c):
                if c < row.R:
                    dve.wait_ge(loaded_in[row.loaded_slot(c)], row.loaded_uses(c) * 16 + 16)
                    dve.wait_ge(pT_done, (i - 1) * CHUNKS + c + 1)
                else:
                    dve.wait_ge(score_done, row.computed0 + c - row.R + 1)
                dve.wait_ge(penalty_made, i * CHUNKS + c + 1)

            STATS0 = GROUPS * GROUP_STATS
            TILE_STATS = 2 + 4

            def step(i, row=None):
                scores, products, layer1 = parts(i, row)
                par = row.par if row else 0
                first = isinstance(i, int) and i == 0
                if scores:
                    make_penalty(i, 0, par)
                for c in range(CHUNKS):
                    if layer1 and c == 1:
                        dve.wait_ge(stats_made, STATS0 + (i - 2) * TILE_STATS + 1)
                    if scores and c == CHUNKS - 1:
                        wait_for_scores(i, row, c)
                    if products:
                        dve.wait_ge(pT_hi_made, (i - 1) * CHUNKS + c + 1)
                        lo_of(pT_lo[:, c % 2].rearrange("p b n -> p (b n)"), pT_ps[c % 2], P_SCALE,
                              pT_hi[:, c % 2].rearrange("p b n -> p (b n)"), pT_lo_made)
                    if layer1 and c == 1:
                        nc.vector.bn_aggr(moments[:, 0, :], stats[:, 0, :]).then_inc(stats_made, 1)
                    if products and c + AHEAD < CHUNKS:
                        times_adj(i - 1, c + AHEAD, 1 - par)
                    if scores and c < CHUNKS - 1:
                        wait_for_scores(i, row, c)
                        make_penalty(i, c + 1, par)
                    if scores:
                        source = loaded[:, row.loaded_slot(c), :] if c < row.R else score_ps[row.score_bank(c)]
                        nc.vector.tensor_tensor_reduce(probs[:, c * CW:(c + 1) * CW], source, penalty[:, c % 2],
                                                       1.0, -3.0e38, ALU.add, ALU.max,
                                                       chunk_max[:, c:c + 1]).then_inc(masked, 1)
                    if layer1 and c == 0:
                        dve.wait_ge(x1_made, i - 1)
                        nc.vector.bn_stats(stats[:, 0, :], x_sb[:, :]).then_inc(stats_made, 1)
                    if layer1 and c == 1:
                        base = STATS0 + (i - 2) * TILE_STATS
                        dve.wait_ge(stats_made, base + 2)
                        nc.vector.tensor_scalar(var_eps[:, 0:1], moments[:, 0, 1:2], EPS, None, ALU.add).then_inc(var_made, 1)
                    if layer1 and c == 3:
                        base = STATS0 + (i - 2) * TILE_STATS
                        dve.wait_ge(rough_made, i - 1 + GROUPS)
                        newton_step(base + 2, 1)
                        wait_from(dve, h1T_done, i - 2)
                        nc.vector.tensor_scalar(h1_sb[:, :], x_sb[:, :], moments[:, 0, 0:1], rstd[:, 0:1],
                                                ALU.subtract, ALU.mult).then_inc(h1_made, 1)
                    if layer1 and c == 6:
                        dve.wait_ge(h1T_hi_made, i - 1)
                        nc.vector.scalar_tensor_tensor(out=h1T[:, 1].rearrange("p k n -> p (k n)"), in0=h1T_ps, scalar=0.0,
                                                       in1=h1T[:, 0].rearrange("p k n -> p (k n)"),
                                                       op0=ALU.max, op1=ALU.subtract).then_inc(h1T_lo_made, 1)
                    if first and c == 2:
                        dve.wait_ge(node_row_done, 1)
                        nc.vector.tensor_reduce(out=node_neg[:, :], in_=y_ps[:, 0:P], axis=AX.X, op=ALU.max,
                                                negate=True).then_inc(node_step, 1)
                    if first and c == 6:
                        dve.wait_ge(node_total_done, 1)
                        nc.vector.reciprocal(node_rec[:, :], y_ps[:, 0:1]).then_inc(node_step, 1)
                        dve.wait_ge(node_step, 4)
                        nc.vector.tensor_scalar(node_att[:, :], node_att[:, :], node_rec[:, :], 1.0 / (P_SCALE * S_SCALE),
                                                ALU.mult, ALU.mult).then_inc(node_step, 1)
                if scores:
                    dve.wait_ge(masked, i * CHUNKS + CHUNKS)
                    nc.vector.tensor_reduce(out=row_max[:, :], in_=chunk_max[:, :], axis=AX.X, op=ALU.max).then_inc(max_step, 1)
                    dve.wait_ge(max_step, i * 2 + 1)
                    nc.vector.tensor_scalar(neg_max[:, :], row_max[:, :], -1.0 / E_SCALE, None, ALU.mult).then_inc(max_step, 1)
                    for c in range(AHEAD):
                        times_adj(i, c, par)
                if layer1:
                    dve.wait_ge(y_hi_made, i - 1)
                    lo_of(y_out[:, 1], y_ps, Y_SCALE / (H_SCALE * W_SCALE), y_out[:, 0], y_lo_made)
                if products:
                    base = (i - 1) * 3
                    if isinstance(i, int) and i == 1:
                        dve.wait_ge(node_step, 5)
                    nc.vector.reduce_sum(out=row_sum[:, :], in_=chunk_sum[:, 1 - par, :], axis=AX.X).then_inc(sum_step, 1)
                    dve.wait_ge(sum_step, base + 1)
                    nc.vector.reciprocal(row_rec[:, :], row_sum[:, :]).then_inc(sum_step, 1)
                    dve.wait_ge(sum_step, base + 2)
                    nc.vector.tensor_tensor(row_fac[:, :], row_rec[:, :], node_att[:, bass.ds(i - 1, 1)], ALU.mult).then_inc(sum_step, 1)
                    dve.wait_ge(sum_step, base + 3)
                    dve.wait_ge(xb_made, i)
                    dve.wait_ge(att_done, i * CHUNKS)
                    nc.vector.scalar_tensor_tensor(out=x_sb[:, :], in0=att_ps, scalar=row_fac[:, :], in1=x_sb[:, :],
                                                   op0=ALU.mult, op1=ALU.add).then_inc(x1_made, 1)

            steps(dve, step)
            step(TILES)
            step(TILES + 1)

            with dve.Fori(0, GROUPS // 2) as s:
                for slot in range(2):
                    dve.wait_ge(x1_in[slot], s * 16 + 16)
                    for t in range(GT):
                        dve.wait_ge(relu_made, (s * 2 + slot) * GT + t + 1)
                        nc.vector.tensor_tensor(out_grp[:, slot, t], out_grp[:, slot, t], x1_grp[:, slot, t],
                                                ALU.add).then_inc(out_made, 1)

        @block.tensor
        def _(pe):
            def product(bank, stationary, moving, done):
                for k in range(KD):
                    for n, (a, b) in enumerate(((0, 0), (0, 1), (1, 0))):
                        last = nc.tensor.matmul(bank, stationary(a, k), moving(b, k), start=(k == 0 and n == 0),
                                                stop=(k == KD - 1 and n == 2))
                last.then_inc(done, 1)

            def transposed(bank, block_of, done, identity=ident):
                for b in range(BPC):
                    last = nc.tensor.transpose(bank[:, b * P:(b + 1) * P], block_of(b), identity[:, :])
                last.then_inc(done, 1)

            def transpose_h(g, k, slot):
                pe.wait_ge(h_made, g * GT + GT)
                wait_from(pe, hT_lo_made, g * KD + k - 1)
                transposed(hT_ps[k % 2], lambda t: hg[:, slot, t, k * P:(k + 1) * P], hT_done)

            def project(g, slot, ahead):
                for m in range(KD):
                    if ahead:
                        transpose_h(g + 1, m, 1 - slot)
                    if m == 0:
                        pe.wait_ge(hT_lo_made, g * KD + KD)
                    wait_from(pe, g_lo_made, g * KD + m - 1)
                    product(g_ps[m % 2], lambda a, k: edge_hl[:, a, k, m * P:(m + 1) * P],
                            lambda b, k: hT[:, slot, b, k, :], g_done)
                if isinstance(g, int) and g == 0:
                    pe.wait_ge(w_lo_made, 3)
                wait_from(pe, logits_made, g)
                for t in range(GT):
                    wait_from(pe, s_lo_made, g * GT + t - 1)
                    rows = slice(t * P, (t + 1) * P)
                    product(s_ps[t % 2], lambda a, k: hT[:, slot, a, k, rows], lambda b, k: w_hl[:, b, k, :], s_done)
                    for k in range(KD):
                        for n, (a, b) in enumerate(((0, 0), (0, 1), (1, 0))):
                            last = nc.tensor.matmul(node_ps[:, t:t + 1], hT[:, slot, a, k, rows], node_hl[:, b, k:k + 1],
                                                    start=(k == 0 and n == 0), stop=(k == KD - 1 and n == 2))
                last.then_inc(node_done, 1)

            pe.wait_ge(ident_made, 3)
            for k in range(KD):
                transpose_h(0, k, 0)
            pe.wait_ge(w_lo_made, 1)
            project(0, 0, True)
            with pe.Fori(0, (GROUPS - 2) // 2) as s:
                project(s * 2 + 1, 1, True)
                project(s * 2 + 2, 0, True)
            project(GROUPS - 1, 1, False)

            def transpose_scores(row, c):
                m = row.moved0 + c - row.R - 1
                pe.wait_ge(raw_made, m + 1)
                wait_from(pe, scoresT_made, m)
                transposed(scoresT_ps, lambda b: raw[:, row.moved_slot(c), b * P:(b + 1) * P], scoresT_done)

            def add_products(i, c):
                n = (i - 1) * CHUNKS + c
                pe.wait_ge(pT_lo_made, n + 1)
                if c == 0:
                    wait_from(pe, x1_made, i - 1)
                for b in range(BPC):
                    j = c * BPC + b
                    for m, (pT, s) in enumerate(((pT_hi, s_hi), (pT_hi, s_lo), (pT_lo, s_hi))):
                        last = nc.tensor.matmul(att_ps, pT[:, c % 2, b, :], s[:, j, :], start=(j == 0 and m == 0),
                                                stop=(j == TILES - 1 and m == 2))
                last.then_inc(att_done, 1)

            def step(i, row=None):
                scores, products, layer1 = parts(i, row)
                par = row.par if row else 0
                first = isinstance(i, int) and i == 0
                for c in range(CHUNKS):
                    if products:
                        n = (i - 1) * CHUNKS + c
                        pe.wait_ge(probs_made, n + 1)
                        wait_from(pe, pT_lo_made, n - 1)
                        transposed(pT_ps[c % 2], lambda b: probs[:, c * CW + b * P:c * CW + (b + 1) * P], pT_done)
                    if scores and c >= row.R:
                        k = c - row.R
                        if k == 0:
                            pe.wait_ge(g_cur_made, i * 2 + 2)
                        wait_from(pe, masked, i * CHUNKS + (c - 1 if k >= 2 else 0))
                        wait_from(pe, raw_made, row.moved0 + (k - 2 if k >= 2 else 0))
                        product(score_ps[row.score_bank(c)], lambda a, k: g_cur[:, a, k, :],
                                lambda b, k: (gT_hi, gT_lo)[b][:, k, c * CW:(c + 1) * CW], score_done)
                        if k >= 2:
                            transpose_scores(row, c - 1)
                    if scores:
                        pe.wait_ge(adj_16_made, i * CHUNKS + c + 1)
                        wait_from(pe, adjT_made, i * CHUNKS + c)
                        transposed(adjT_ps, lambda b: adj_16[:, c % 2, b * P:(b + 1) * P], adjT_done, ident_16)
                    if layer1 and c == 5:
                        pe.wait_ge(h1_made, i - 1)
                        wait_from(pe, y_lo_made, i - 2)
                        transposed(h1T_ps, lambda k: h1_sb[:, k * P:(k + 1) * P], h1T_done)
                    if layer1 and c == 7:
                        pe.wait_ge(h1T_lo_made, i - 1)
                        product(y_ps, lambda a, k: h1T[:, a, k, :], lambda b, k: w1_hl[:, b, k, :], y_done)
                    if first and c == 0:
                        pe.wait_ge(node_step, 2)
                        nc.tensor.matmul(y_ps[:, 0:P], node_row[:, :], ident[:, :], start=True, stop=True).then_inc(node_row_done, 1)
                    if first and c == 5:
                        pe.wait_ge(node_exp_made, 1)
                        nc.tensor.matmul(y_ps[:, 0:1], ones[:, :], node_sum[:, :], start=True, stop=True).then_inc(node_total_done, 1)
                    if products and c >= 1:
                        add_products(i, c - 1)
                if scores and row.R < CHUNKS - 1:
                    transpose_scores(row, CHUNKS - 1)
                if products:
                    add_products(i, CHUNKS - 1)

            pe.wait_ge(s_lo_made, TILES)
            steps(pe, step)
            step(TILES)
            step(TILES + 1)

            def group(G, slot, first=False):
                for j in range(TILES):
                    if first:
                        for n, (a, b) in enumerate(Y_LOADS):
                            if j == a:
                                pe.wait_ge(y_in[n], 32)
                    for t in range(GT):
                        for m, y in enumerate((y_hi, y_lo)):
                            last = nc.tensor.matmul(banks[:, slot * GT + t, :], adjT_grp[slot][:, t, j * P:(j + 1) * P],
                                                    y[:, j, :], start=(j == 0 and m == 0), stop=(j == TILES - 1 and m == 1))
                        if j == TILES - 1:
                            last.then_inc(z_done, 1)

            pe.wait_ge(adjT_in[0], 16)
            group(0, 0, first=True)
            pe.wait_ge(adjT_in[1], 16)
            group(1, 1)
            with pe.Fori(1, GROUPS // 2) as s:
                for slot in range(2):
                    pe.wait_ge(adjT_in[slot], s * 16 + 16)
                    pe.wait_ge(relu_made, (s * 2 + slot - 1) * GT)
                    group(s * 2 + slot, slot)


_INS = ["x", "adj", "L0_gnn_weight", "L0_gnn_bias", "L0_gnn_node_w", "L0_gnn_edge_w", "L1_gnn_weight"]


def kernel(**inputs):
    import concourse.bacc as bacc
    from concourse.bass_utils import run_bass_kernel_spmd

    nc = bacc.Bacc("TRN2", target_bir_lowering=False, num_devices=1, dynamic_dma_scratch_size=1024)
    arrays, args = {}, []
    for name in _INS:
        a = np.ascontiguousarray(inputs[name])
        arrays[f"in_{name}"] = a
        args.append(nc.dram_tensor(f"in_{name}", a.shape, mybir.dt.from_np(a.dtype), kind="ExternalInput").ap())
    out = nc.dram_tensor("out", (N, D), mybir.dt.float32, kind="ExternalOutput").ap()
    build_program(nc, *args, out)
    results = run_bass_kernel_spmd(nc, [arrays], core_ids=[0])
    return results.results[0]["out"]
```

```python
from contextlib import ExitStack

import concourse.bass as bass
from concourse import mybir
import numpy as np

P = 128
N, D = 4096, 512
TILES = N // P
KD = D // P
CW = 512
CHUNKS = N // CW
BPC = CW // P
GT = 4
GROUPS = TILES // GT
EPS = 1e-5
NEG_BIG = -9000000000000000.0

H_SCALE = 64.0
W_SCALE = 64.0
G_SCALE = 8.0
S_SCALE = 16.0
P_SCALE = 256.0
Y_SCALE = 64.0
E_SCALE = G_SCALE * G_SCALE


AHEAD = 2
SUPER = CW // P
SUPERS = TILES // SUPER


class Row:

    def __init__(self, R, s, par):
        self.R, self.s, self.par = R, s, par
        self.tile = s * 2 + (SUPER * R + par)
        self.last = isinstance(s, int) and self.tile == TILES - 1
        computed, moved = CHUNKS - R, CHUNKS - 1 - R
        self.computed0 = s * (2 * computed) + (sum(SUPER * (CHUNKS - r) for r in range(R)) + par * computed)
        self.moved0 = s * (2 * moved) + (sum(SUPER * (CHUNKS - 1 - r) for r in range(R)) + par * moved)
        self.moved_half = s * moved + sum(SUPER // 2 * (CHUNKS - 1 - r) for r in range(R))
        self.loaded_half = s * R + sum(SUPER // 2 * r for r in range(R))

    def next(self):
        return Row(self.R, self.s, 1) if self.par == 0 else Row(self.R, self.s + 1, 0)

    def score_bank(self, c):
        return (self.par * (CHUNKS - self.R) + c - self.R) % 2

    def moved_slot(self, c):
        return (self.par * (CHUNKS - 1 - self.R) + c - self.R - 1) % 2

    def moved_uses(self, c):
        return self.moved_half + (self.par * (CHUNKS - 1 - self.R) + c - self.R - 1) // 2

    def loaded_slot(self, c):
        return (self.par * self.R + c) % 2

    def loaded_uses(self, c):
        return self.loaded_half + (self.par * self.R + c) // 2


def wait_from(engine, semaphore, value):
    if isinstance(value, int) and value <= 0:
        return
    engine.wait_ge(semaphore, value)


def build_program(nc, x, adj, weight, bias, node_w, edge_w, weight1, out):
    f32, f16 = mybir.dt.float32, mybir.dt.float16
    ALU, ACT, AX = mybir.AluOpType, mybir.ActivationFunctionType, mybir.AxisListType

    adj_16_dram = nc.dram_tensor("adj_16_scratch", (TILES, P, 2 * N), f16, kind="Internal").ap()[:, :, 0:N]
    y_dram = nc.dram_tensor("y_scratch", (TILES, P, 2, D), f16, kind="Internal").ap()
    scores_dram = nc.dram_tensor("scores_scratch", (TILES, P, N), f32, kind="Internal").ap()
    x1_dram = nc.dram_tensor("x1_scratch", (TILES, P, D), f32, kind="Internal").ap()

    x_groups = x.rearrange("(g t p) d -> g p t d", t=GT, p=P)
    x_tiles = x.rearrange("(t p) d -> t p d", p=P)
    adj_tiles = adj.rearrange("(t p) n -> t p n", p=P)
    out_tiles = out.rearrange("(t p) d -> t p d", p=P)

    with ExitStack() as ctx:
        def sb(name, shape, dt):
            return ctx.enter_context(nc.sbuf_tensor(name, shape, dt))

        def sem(name):
            return ctx.enter_context(nc.semaphore(name))

        gT_hi = sb("gT_hi", [P, KD, N], f16)
        gT_lo = sb("gT_lo", [P, KD, N], f16)
        s_hi = sb("s_hi", [P, TILES, D], f16)
        s_lo = sb("s_lo", [P, TILES, D], f16)
        probs = sb("probs", [P, N], f32)
        adj_sb = sb("adj_sb", [P, 2, N], f32)
        w1_hl = sb("w1_hl", [P, 2, KD, D], f16)
        shared = sb("shared", [P, 8192], f16)
        g_even = sb("g_even", [P, 2, KD, P], f16)
        x_sb = sb("x_sb", [P, D], f32)
        scoresT_sb = sb("scoresT_sb", [P, 2, BPC, P], f32)
        loaded = sb("loaded", [P, 2, CW], f32)
        h1_sb = sb("h1_sb", [P, D], f32)
        h1T = sb("h1T", [P, 2, KD, P], f16)
        y_out = sb("y_out", [P, 2, D], f16)
        bias_sb = sb("bias_sb", [P, D], f32)
        ident = sb("ident", [P, P], f32)
        ones = sb("ones", [P, P], f32)
        half = sb("half", [P, GT], f32)
        logits = sb("logits", [P, TILES], f32)
        node_att = sb("node_att", [P, TILES], f32)
        node_col = sb("node_col", [P, 1], f32)
        node_neg = sb("node_neg", [P, 1], f32)
        node_sum = sb("node_sum", [P, 1], f32)
        node_rec = sb("node_rec", [P, 1], f32)
        node_row = loaded[:, 0, 0:P]
        node_products = loaded[:, 1, :]
        node_w_sb = h1_sb
        stats = sb("stats", [P, GT, 6], f32)
        moments = sb("moments", [P, GT, 2], f32)
        var_eps = sb("var_eps", [P, GT], f32)
        rough = sb("rough", [P, GT], f32)
        newton = sb("newton", [P, GT], f32)
        rstd = sb("rstd", [P, GT], f32)
        chunk_max = sb("chunk_max", [P, CHUNKS], f32)
        row_max = sb("row_max", [P, 1], f32)
        neg_max = sb("neg_max", [P, 1], f32)
        chunk_sum = sb("chunk_sum", [P, 2, CHUNKS], f32)
        row_sum = sb("row_sum", [P, 1], f32)
        row_rec = sb("row_rec", [P, 1], f32)
        row_fac = sb("row_fac", [P, 1], f32)
        odd_chunk = sb("odd_chunk", [P, CHUNKS], f32)
        odd_tile = sb("odd_tile", [P, TILES], f32)
        odd_row = sb("odd_row", [P, 1], f32)
        odd_count = sb("odd_count", [P, 1], mybir.dt.int32)

        edge_hl = shared[:, 0:4096].rearrange("p (h k n) -> p h k n", h=2, k=KD)
        w_hl = shared[:, 4096:8192].rearrange("p (h k n) -> p h k n", h=2, k=KD)
        hT = probs[:, :].bitcast(f16).rearrange("p (s h k n) -> p s h k n", s=2, h=2, k=KD)
        xg = adj_sb[:, 0, :].rearrange("p (s t d) -> p s t d", s=2, t=GT)
        hg = adj_sb[:, 1, :].rearrange("p (s t d) -> p s t d", s=2, t=GT)
        stage_edge = s_lo[:, 24:32, :].rearrange("p a b -> p (a b)").bitcast(f32)
        stage_w = s_hi[:, 24:32, :].rearrange("p a b -> p (a b)").bitcast(f32)
        stage_w1 = s_hi[:, 16:24, :].rearrange("p a b -> p (a b)").bitcast(f32)
        penalty = shared[:, 0:1024].bitcast(mybir.dt.bfloat16).rearrange("p (s n) -> p s n", s=2)
        g_cur = [g_even, shared[:, 1024:2048].rearrange("p (h k n) -> p h k n", h=2, k=KD)]
        pT_hi = shared[:, 2048:3072].rearrange("p (s b n) -> p s b n", s=2, b=BPC)
        pT_lo = shared[:, 3072:4096].rearrange("p (s b n) -> p s b n", s=2, b=BPC)
        adj_16 = shared[:, 4096:6144].rearrange("p (s n) -> p s n", s=2)
        raw = shared[:, 6144:8192].bitcast(f32).rearrange("p (s n) -> p s n", s=2)
        y_hi = gT_hi[:, :, :].rearrange("p k n -> p (k n)").rearrange("p (j d) -> p j d", d=D)
        y_lo = gT_lo[:, :, :].rearrange("p k n -> p (k n)").rearrange("p (j d) -> p j d", d=D)
        adjT_grp = [adj_sb[:, :, :].rearrange("p s n -> p (s n)").bitcast(f16).rearrange("p (t n) -> p t n", t=GT),
                    s_hi[:, :, :].rearrange("p j d -> p (j d)").rearrange("p (t n) -> p t n", t=GT)]
        x1_grp = probs[:, :].rearrange("p (s t d) -> p s t d", s=2, t=GT)
        out_grp = s_lo[:, :, :].rearrange("p j d -> p (j d)").bitcast(f32).rearrange(
            "p (s t d) -> p s t d", s=4, t=GT)

        exact_adj = adj_sb[:, 0, :]
        exact_adjT = adj_sb[:, 1, :]
        exact_y = [s_hi[:, :, :].rearrange("p j d -> p (j d)").bitcast(f32).rearrange("p (j d) -> p j d", d=D),
                   s_lo[:, :, :].rearrange("p j d -> p (j d)").bitcast(f32).rearrange("p (j d) -> p j d", d=D)]
        exact_x1, exact_out = probs[:, 0:D], probs[:, D:2 * D]

        banks = ctx.enter_context(nc.psum_tensor("banks", [P, 8, 512], f32))
        hT_ps = [banks[:, b, :] for b in (0, 1)]
        g_ps = [banks[:, b, :] for b in (2, 3)]
        s_ps = [banks[:, b, :] for b in (4, 5)]
        score_ps = [banks[:, b, :] for b in (0, 1)]
        pT_ps = [banks[:, b, :] for b in (2, 3)]
        att_ps = [banks[:, b, :] for b in (4, 5)]
        h1T_ps = y_ps = banks[:, 6, :]
        scoresT_ps = banks[:, 7, :]

        ident_made = sem("ident_made")
        ones_made = sem("ones_made")
        edge_in = sem("edge_in")
        weight_in = sem("weight_in")
        w1_in = sem("w1_in")
        node_in = sem("node_in")
        bias_in = sem("bias_in")
        w_hi_made = sem("w_hi_made")
        w_lo_made = sem("w_lo_made")
        xg_in = [sem("xg_in0"), sem("xg_in1")]
        stats_made = sem("stats_made")
        var_made = sem("var_made")
        rough_made = sem("rough_made")
        h_made = sem("h_made")
        hT_done = sem("hT_done")
        hT_hi_made = sem("hT_hi_made")
        hT_lo_made = sem("hT_lo_made")
        g_done = sem("g_done")
        g_hi_made = sem("g_hi_made")
        g_lo_made = sem("g_lo_made")
        s_done = sem("s_done")
        s_hi_made = sem("s_hi_made")
        s_lo_made = sem("s_lo_made")
        logits_made = sem("logits_made")
        node_step = sem("node_step")
        node_row_done = sem("node_row_done")
        node_exp_made = sem("node_exp_made")
        node_total_done = sem("node_total_done")
        adj_in = [[sem("adj_in00"), sem("adj_in01")], [sem("adj_in10"), sem("adj_in11")]]
        x_in = sem("x_in")
        xb_made = sem("xb_made")
        g_cur_made = sem("g_cur_made")
        penalty_made = sem("penalty_made")
        score_done = sem("score_done")
        masked = sem("masked")
        raw_made = sem("raw_made")
        scoresT_done = sem("scoresT_done")
        scoresT_made = sem("scoresT_made")
        scoresT_out = [sem("scoresT_out0"), sem("scoresT_out1")]
        loaded_in = [sem("loaded_in0"), sem("loaded_in1")]
        max_step = sem("max_step")
        exp_made = sem("exp_made")
        probs_made = sem("probs_made")
        pT_done = sem("pT_done")
        pT_hi_made = sem("pT_hi_made")
        pT_lo_made = sem("pT_lo_made")
        att_done = sem("att_done")
        adj_16_made = sem("adj_16_made")
        adj_16_out = [sem("adj_16_out0"), sem("adj_16_out1")]
        sum_step = sem("sum_step")
        x1_made = sem("x1_made")
        x1_out = sem("x1_out")
        h1_made = sem("h1_made")
        h1T_done = sem("h1T_done")
        h1T_hi_made = sem("h1T_hi_made")
        h1T_lo_made = sem("h1T_lo_made")
        y_done = sem("y_done")
        y_hi_made = sem("y_hi_made")
        y_lo_made = sem("y_lo_made")
        y_stored = sem("y_stored")
        y_in_early = sem("y_in_early")
        y_in_late = sem("y_in_late")
        adjT_in_first = [sem(f"adjT_in_first{t}") for t in range(GT)]
        adjT_in = [sem("adjT_in0"), sem("adjT_in1")]
        x1_in = [sem("x1_in0"), sem("x1_in1")]
        z_done = sem("z_done")
        relu_made = sem("relu_made")
        out_made = sem("out_made")
        out_stored = [sem("out_stored0"), sem("out_stored1")]

        odd_made = sem("odd_made")
        odd_tile_made = sem("odd_tile_made")
        odd_row_made = sem("odd_row_made")
        odd_total_done = sem("odd_total_done")
        odd_count_made = sem("odd_count_made")
        exact_y_made = sem("exact_y_made")
        exact_adj_in = sem("exact_adj_in")
        exact_x1_in = sem("exact_x1_in")
        exact_adjT_done = sem("exact_adjT_done")
        exact_adjT_made = sem("exact_adjT_made")
        exact_z_done = sem("exact_z_done")
        exact_relu_made = sem("exact_relu_made")
        exact_out_made = sem("exact_out_made")
        exact_stored = sem("exact_stored")

        block = ctx.enter_context(nc.Block())

        def steps(engine, step, unroll_last=False, before=None):
            for par in range(2):
                step(par, Row(0, 0, par))
            for par in range(2):
                step(2 + par, Row(0, 1, par))
            for R in range(1, SUPERS):
                if before:
                    before(R)
                if unroll_last and R == SUPERS - 1:
                    for s in range(SUPER // 2):
                        for par in range(2):
                            row = Row(R, s, par)
                            step(row.tile, row)
                else:
                    with engine.Fori(0, SUPER // 2) as s:
                        for par in range(2):
                            row = Row(R, s, par)
                            step(row.tile, row)

        def parts(i, row):
            if isinstance(i, int):
                return row is not None, 1 <= i <= TILES, i >= 2
            return True, True, True

        @block.sync
        def _(sp):
            sp.dma_start(xg[:, 0], x_groups[0]).then_inc(xg_in[0], 16)
            sp.dma_start(stage_edge.rearrange("p (k n) -> p k n", k=KD),
                         edge_w.rearrange("(k p) n -> p k n", p=P)).then_inc(edge_in, 16)
            sp.dma_start(xg[:, 1], x_groups[1]).then_inc(xg_in[1], 16)
            sp.dma_start(stage_w.rearrange("p (k n) -> p k n", k=KD),
                         weight.rearrange("(k p) n -> p k n", p=P)).then_inc(weight_in, 16)
            sp.dma_start(node_w_sb[:, :], node_w.rearrange("n o -> o n").to_broadcast((P, D))).then_inc(node_in, 16)
            sp.dma_start(stage_w1.rearrange("p (k n) -> p k n", k=KD),
                         weight1.rearrange("(k p) n -> p k n", p=P)).then_inc(w1_in, 16)
            sp.dma_start(bias_sb[:, :], bias.rearrange("(o n) -> o n", o=1).to_broadcast((P, D))).then_inc(bias_in, 16)
            with sp.Fori(0, (GROUPS - 2) // 2) as s:
                for half_ in range(2):
                    g = s * 2 + half_
                    sp.wait_ge(h_made, g * GT + GT)
                    sp.dma_start(xg[:, half_], x_groups[bass.ds(g + 2, 1)].rearrange("o p t d -> (o p) t d")
                                 ).then_inc(xg_in[half_], 16)

            def load_adj(i, slot, hf):
                cols = slice(hf * N // 2, (hf + 1) * N // 2)
                sp.dma_start(adj_sb[:, slot, cols], adj_tiles[bass.ds(i, 1), :, cols].rearrange("o p n -> (o p) n")
                             ).then_inc(adj_in[slot][hf], 16)

            def load_x(i):
                sp.dma_start(x_sb[:, :], x_tiles[bass.ds(i, 1)].rearrange("o p d -> (o p) d")).then_inc(x_in, 16)

            sp.wait_ge(h_made, TILES)
            load_adj(0, 0, 0)
            load_adj(0, 0, 1)
            load_x(0)

            def load_scores(row, c):
                i = row.tile
                sp.wait_ge(masked, i * CHUNKS + (c - 1 if c >= 2 else 0))
                sp.dma_start(loaded[:, row.loaded_slot(c), :],
                             scores_dram[bass.ds(i, 1), :, c * CW:(c + 1) * CW].rearrange("o p n -> (o p) n")
                             ).then_inc(loaded_in[row.loaded_slot(c)], 16)

            def store_scoresT(row, c):
                slot = row.moved_slot(c)
                sp.wait_ge(scoresT_made, row.moved0 + c - row.R)
                sp.dma_start(scores_dram[c * BPC:(c + 1) * BPC, :, bass.ds(row.tile * P, P)].rearrange("b p n -> p b n"),
                             scoresT_sb[:, slot]).then_inc(scoresT_out[slot], 16)

            def store_y(y):
                sp.wait_ge(y_lo_made, y + 1)
                sp.dma_start(y_dram[bass.ds(y, 1)].rearrange("o p h d -> (o p) h d"), y_out[:, :, :]).then_inc(y_stored, 16)

            def store_adj_16(i, pair):
                sp.wait_ge(adj_16_made, i * CHUNKS + 2 * pair + 2)
                sp.dma_start(adj_16_dram[bass.ds(i, 1), :, pair * 2 * CW:(pair + 1) * 2 * CW].rearrange("o p n -> (o p) n"),
                             adj_16[:, pair % 2, :]).then_inc(adj_16_out[pair % 2], 16)

            def before_super_row(R):
                for sl in range(2):
                    sp.wait_ge(scoresT_out[sl], 16 * sum(SUPER // 2 * (CHUNKS - 1 - r) for r in range(R)))
                if R == SUPERS - 1:
                    sp.wait_ge(score_done, SUPER * sum(CHUNKS - r for r in range(SUPERS - 1)))
                    sp.wait_ge(y_stored, (TILES - CHUNKS) * 16)
                if R <= 2:
                    load_scores(Row(R, 0, 0), R - 1)

            def load_y_early(j):
                for hl, to in ((0, y_hi), (1, y_lo)):
                    sp.dma_start(to[:, j, :], y_dram[j, :, hl, :]).then_inc(y_in_early, 16)

            def step(i, row=None):
                scores, products, layer1 = parts(i, row)
                R = row.R if row else 0
                if layer1:
                    sp.wait_ge(x1_made, i - 1)
                    sp.dma_start(x1_dram[bass.ds(i - 2, 1)].rearrange("o p d -> (o p) d"), x_sb[:, :]).then_inc(x1_out, 16)
                if scores and not products:
                    sp.wait_ge(hT_done, GROUPS * KD)
                    sp.wait_ge(logits_made, TILES)
                    load_adj(1, 1, 0)
                    load_adj(1, 1, 1)
                for c in range(2, CHUNKS):
                    if scores and products and not row.last and c in (4, 7):
                        sp.wait_ge(probs_made, i * CHUNKS - (4 if c == 4 else 0))
                        load_adj(i + 1, 1 - row.par, 0 if c == 4 else 1)
                    if scores and c < R:
                        load_scores(row, c)
                    if scores and R == SUPERS - 1 and not row.last:
                        for n in (0, 1) if c == 2 else (c - 1,):
                            load_y_early((i - R * SUPER) * CHUNKS + n)
                    if scores and c > R + 1:
                        store_scoresT(row, c - 1)
                    if scores and c % 2 == 0:
                        store_adj_16(i, c // 2 - 1)
                    if layer1 and products and c == 5:
                        sp.wait_ge(x1_out, (i - 1) * 16)
                        sp.wait_ge(h1_made, i - 1)
                        load_x(i - 1)
                if scores and not row.last:
                    for c in range(min(R, 2)):
                        load_scores(row.next(), c)
                if scores and R < CHUNKS - 1:
                    store_scoresT(row, CHUNKS - 1)
                if scores:
                    store_adj_16(i, CHUNKS // 2 - 1)
                if layer1 and scores:
                    store_y(i - 2)

            steps(sp, step, unroll_last=True, before=before_super_row)

            def load_adjT(G, t, slot, arrived):
                sp.dma_start_transpose(adjT_grp[slot][:, t].rearrange("p (j n) -> p j n", n=P),
                                       adj_16_dram[bass.ds(G * GT + t, 1)].rearrange("o p n -> (o p) n")).then_inc(arrived, 16)

            def load_x1(G, slot):
                sp.dma_start(x1_grp[:, slot], x1_dram[bass.ds(G * GT, GT)].rearrange("t p d -> p t d")).then_inc(x1_in[slot], 16)

            sp.wait_ge(score_done, SUPER * sum(CHUNKS - R for R in range(SUPERS)))
            sp.wait_ge(y_stored, (TILES - 2) * 16)
            for hl, to in ((0, y_hi), (1, y_lo)):
                sp.dma_start(to[:, CHUNKS - 1:TILES - CHUNKS:CHUNKS, :],
                             y_dram[CHUNKS - 1:TILES - CHUNKS:CHUNKS, :, hl, :].rearrange("j p d -> p j d")).then_inc(y_in_late, 16)
                sp.dma_start(to[:, TILES - CHUNKS:TILES - 2, :],
                             y_dram[TILES - CHUNKS:TILES - 2, :, hl, :].rearrange("j p d -> p j d")).then_inc(y_in_late, 16)
            for sl in range(2):
                sp.wait_ge(adj_16_out[sl], TILES * 2 * 16)
            sp.wait_ge(probs_made, (TILES - 1) * CHUNKS)
            load_adjT(0, 0, 0, adjT_in_first[0])
            step(TILES)
            load_adjT(0, 1, 0, adjT_in_first[1])
            sp.wait_ge(probs_made, TILES * CHUNKS)
            load_adjT(0, 2, 0, adjT_in_first[2])
            load_adjT(0, 3, 0, adjT_in_first[3])
            step(TILES + 1)
            sp.wait_ge(att_done, TILES * CHUNKS)
            for t in range(GT):
                load_adjT(1, t, 1, adjT_in[1])
            sp.wait_ge(x1_out, TILES * 16)
            load_x1(0, 0)
            load_x1(1, 1)

            def group(G, slot, ahead):
                for t in range(GT):
                    if ahead:
                        sp.wait_ge(z_done, G * GT + t + 1)
                        load_adjT(G + 2, t, slot, adjT_in[slot])
                    sp.wait_ge(out_made, G * GT + t + 1)
                    sp.dma_start(out_tiles[bass.ds(G * GT + t, 1)].rearrange("o p d -> (o p) d"),
                                 out_grp[:, slot, t]).then_inc(out_stored[slot], 16)
                if ahead:
                    load_x1(G + 2, slot)

            with sp.Fori(0, GROUPS // 2 - 1) as s:
                group(s * 2, 0, True)
                group(s * 2 + 1, 1, True)
            group(GROUPS - 2, 0, False)
            group(GROUPS - 1, 1, False)
            for sl in range(2):
                sp.wait_ge(out_stored[sl], GROUPS // 2 * GT * 16)

            sp.wait_ge(odd_count_made, 1)
            with sp.If(sp.value_load(odd_count[0:1, 0:1]) > 0):
                with sp.Fori(0, TILES) as i:
                    sp.wait_ge(exact_adjT_done, i * CHUNKS)
                    sp.dma_start(exact_adj, adj_tiles[bass.ds(i, 1)].rearrange("o p n -> (o p) n")).then_inc(exact_adj_in, 16)
                    sp.wait_ge(exact_stored, i * 16)
                    sp.dma_start(exact_x1, x1_dram[bass.ds(i, 1)].rearrange("o p d -> (o p) d")).then_inc(exact_x1_in, 16)
                    sp.wait_ge(exact_out_made, i + 1)
                    sp.dma_start(out_tiles[bass.ds(i, 1)].rearrange("o p d -> (o p) d"), exact_out).then_inc(exact_stored, 16)
                sp.wait_ge(exact_stored, TILES * 16)
            with sp.Else():
                sp.wait_ge(odd_count_made, 1)

        @block.gpsimd
        def _(pool):
            nc.gpsimd.memset(ident[:, :], 0.0).then_inc(ident_made, 1)
            pool.wait_ge(ident_made, 1)
            nc.gpsimd.affine_select(out=ident[:, :], in_=ident[:, :], compare_op=ALU.not_equal, fill=1.0,
                                    base=0, pattern=[[-1, P]], channel_multiplier=1).then_inc(ident_made, 1)
            nc.gpsimd.memset(half[:, :], -0.5).then_inc(ones_made, 1)
            nc.gpsimd.memset(ones[:, :], 1.0).then_inc(ones_made, 1)
            pool.wait_ge(ones_made, 2)
            with pool.Fori(0, GROUPS) as g:
                pool.wait_ge(var_made, g + 1)
                nc.gpsimd.tensor_tensor(rough[:, :], var_eps[:, :], half[:, :], ALU.pow).then_inc(rough_made, 1)
            pool.wait_ge(bias_in, 16)

            def copy_g(i, par):
                for hl, src in ((0, gT_hi), (1, gT_lo)):
                    nc.gpsimd.tensor_copy(g_cur[par][:, hl], src[:, :, bass.ds(i * P, P)]).then_inc(g_cur_made, 1)

            pool.wait_ge(g_lo_made, GROUPS * KD)
            pool.wait_ge(g_hi_made, GROUPS * KD)
            copy_g(0, 0)

            def cast_adj(i, par, chunks):
                for c in chunks:
                    slot = c // 2 % 2
                    if c % 4 == 0:
                        pool.wait_ge(adj_in[par][c // 4], (i - par) * 8 + 16)
                    if c % 2 == 0:
                        wait_from(pool, adj_16_out[slot], (i * 2 + c // 4) * 16)
                    wait_from(pool, odd_made, i * CHUNKS + c - 3)
                    nc.gpsimd.tensor_tensor(adj_16[:, slot, c % 2 * CW:(c % 2 + 1) * CW], adj_sb[:, par, c * CW:(c + 1) * CW],
                                            ones[:, 0:1].to_broadcast((P, CW)), ALU.mult).then_inc(adj_16_made, 1)

            pool.wait_ge(s_done, TILES)
            copy_g(1, 1)
            cast_adj(0, 0, [0])

            def step(i, row=None):
                scores, products, layer1 = parts(i, row)
                par = row.par if row else 0
                if scores:
                    cast_adj(i, par, range(1, 4))
                if layer1:
                    pool.wait_ge(var_made, i - 1 + GROUPS)
                    nc.gpsimd.tensor_tensor(rough[:, 0:1], var_eps[:, 0:1], half[:, 0:1], ALU.pow).then_inc(rough_made, 1)
                if scores:
                    cast_adj(i, par, range(4, CHUNKS))
                if products:
                    pool.wait_ge(x_in, i * 16)
                    nc.gpsimd.tensor_tensor(x_sb[:, :], x_sb[:, :], bias_sb[:, :], ALU.add).then_inc(xb_made, 1)
                if scores and not row.last:
                    cast_adj(i + 1, 1 - par, [0])
                if scores and not (isinstance(i, int) and i >= TILES - 2):
                    pool.wait_ge(score_done, row.computed0 + CHUNKS - row.R)
                    copy_g(i + 2, par)

            steps(pool, step, unroll_last=True)
            step(TILES)
            step(TILES + 1)

        @block.scalar
        def _(act):
            def hi_of_weight(to, src, arrived):
                act.wait_ge(arrived, 16)
                nc.scalar.activation(to, src, ACT.Copy, scale=W_SCALE).then_inc(w_hi_made, 1)

            hi_of_weight(edge_hl[:, 0].rearrange("p k n -> p (k n)"), stage_edge, edge_in)

            def hT_hi(g, k, slot):
                act.wait_ge(hT_done, g * KD + k + 1)
                wait_from(act, s_done, (g - 1) * GT)
                nc.scalar.activation(hT[:, slot, 0, k], hT_ps[k % 2], ACT.Relu).then_inc(hT_hi_made, 1)

            def project(g, slot, ahead):
                first = isinstance(g, int) and g == 0
                for m in range(KD):
                    if ahead and not first:
                        hT_hi(g + 1, m, 1 - slot)
                    act.wait_ge(g_done, g * KD + m + 1)
                    nc.scalar.activation(gT_hi[:, m, bass.ds(g * CW, CW)], g_ps[m % 2], ACT.Copy,
                                         scale=G_SCALE / (H_SCALE * W_SCALE)).then_inc(g_hi_made, 1)
                for t in range(GT):
                    if first:
                        hT_hi(1, t, 1)
                    act.wait_ge(s_done, g * GT + t + 1)
                    nc.scalar.activation(s_hi[:, bass.ds(g * GT + t, 1)].rearrange("p o d -> p (o d)"), s_ps[t % 2],
                                         ACT.Copy, scale=S_SCALE / (H_SCALE * W_SCALE)).then_inc(s_hi_made, 1)

            for k in range(KD):
                hT_hi(0, k, 0)
            hi_of_weight(w_hl[:, 0].rearrange("p k n -> p (k n)"), stage_w, weight_in)
            project(0, 0, True)
            hi_of_weight(w1_hl[:, 0].rearrange("p k n -> p (k n)"), stage_w1, w1_in)
            with act.Fori(0, (GROUPS - 2) // 2) as s:
                project(s * 2 + 1, 1, True)
                project(s * 2 + 2, 0, True)
            project(GROUPS - 1, 1, False)

            def exp_chunk(c, par):
                piece = probs[:, c * CW:(c + 1) * CW]
                nc.scalar.activation(piece, piece, ACT.Exp, bias=neg_max[:, :], scale=1.0 / E_SCALE,
                                     accum_out=chunk_sum[:, par, c:c + 1]).then_inc(exp_made, 1)

            def copy_scoresT(row, c):
                act.wait_ge(scoresT_done, row.moved0 + c - row.R)
                slot = row.moved_slot(c)
                wait_from(act, scoresT_out[slot], row.moved_uses(c) * 16)
                nc.scalar.activation(scoresT_sb[:, slot].rearrange("p b n -> p (b n)"), scoresT_ps,
                                     ACT.Copy).then_inc(scoresT_made, 1)

            def pT_hi_of(tile, c):
                n = tile * CHUNKS + c
                act.wait_ge(pT_done, n + 1)
                wait_from(act, att_done, n - 1)
                nc.scalar.activation(pT_hi[:, c % 2].rearrange("p b n -> p (b n)"), pT_ps[c % 2], ACT.Copy,
                                     scale=P_SCALE).then_inc(pT_hi_made, 1)

            def step(i, row=None):
                scores, products, layer1 = parts(i, row)
                par = row.par if row else 0
                first = isinstance(i, int) and i == 0
                for c in range(CHUNKS):
                    if products and c != 1:
                        pT_hi_of(i - 1, c if c else 1)
                    if products and c + AHEAD < CHUNKS:
                        exp_chunk(c + AHEAD, 1 - par)
                    if scores and c > row.R:
                        act.wait_ge(masked, i * CHUNKS + c + 1)
                        wait_from(act, scoresT_done, row.moved0 + c - row.R - 2)
                        nc.scalar.activation(raw[:, row.moved_slot(c), :], score_ps[row.score_bank(c)],
                                             ACT.Copy).then_inc(raw_made, 1)
                    if scores and c > row.R + 1:
                        copy_scoresT(row, c - 1)
                    if layer1 and c == 6:
                        act.wait_ge(h1T_done, i - 1)
                        nc.scalar.activation(h1T[:, 0].rearrange("p k n -> p (k n)"), h1T_ps, ACT.Relu).then_inc(h1T_hi_made, 1)
                    if first and c == 4:
                        act.wait_ge(node_step, 4)
                        nc.scalar.activation(node_att[:, :], logits[:, :], ACT.Exp, bias=node_neg[:, :], scale=1.0 / H_SCALE,
                                             accum_out=node_sum[:, :]).then_inc(node_exp_made, 1)
                if scores:
                    act.wait_ge(max_step, i * 2 + 2)
                    for c in range(AHEAD):
                        exp_chunk(c, par)
                    if row.R < CHUNKS - 1:
                        copy_scoresT(row, CHUNKS - 1)
                if layer1:
                    act.wait_ge(y_done, i - 1)
                    if scores:
                        wait_from(act, y_stored, (i - 2) * 16)
                    nc.scalar.activation(y_out[:, 0] if scores else y_hi[:, i - 2], y_ps, ACT.Copy,
                                         scale=Y_SCALE / (H_SCALE * W_SCALE)).then_inc(y_hi_made, 1)
                if scores:
                    pT_hi_of(i, 0)

            steps(act, step)
            step(TILES)
            step(TILES + 1)

            def group(G, slot):
                for t in range(GT):
                    act.wait_ge(z_done, G * GT + t + 1)
                    nc.scalar.activation(out_grp[:, slot, t], banks[:, slot * GT + t, :], ACT.Relu,
                                         scale=1.0 / Y_SCALE).then_inc(relu_made, 1)

            group(0, 0)
            group(1, 1)
            with act.Fori(1, GROUPS // 2) as s:
                for slot in range(2):
                    act.wait_ge(out_stored[slot], s * GT * 16)
                    group(s * 2 + slot, slot)

            act.wait_ge(odd_count_made, 1)
            with act.If(act.value_load(odd_count[0:1, 0:1]) > 0):
                with act.Fori(0, TILES) as i:
                    for c in range(CHUNKS):
                        if c == 0:
                            act.wait_ge(exact_z_done, i)
                        act.wait_ge(exact_adjT_done, i * CHUNKS + c + 1)
                        nc.scalar.activation(exact_adjT[:, c * CW:(c + 1) * CW], banks[:, c % 2, :],
                                             ACT.Copy).then_inc(exact_adjT_made, 1)
                    act.wait_ge(exact_z_done, i + 1)
                    act.wait_ge(exact_stored, i * 16)
                    nc.scalar.activation(exact_out, banks[:, 2, :], ACT.Relu, scale=1.0 / Y_SCALE).then_inc(exact_relu_made, 1)
            with act.Else():
                act.wait_ge(odd_count_made, 1)

        @block.vector
        def _(dve):
            def lo_of(to, src, scale, hi, made):
                nc.vector.scalar_tensor_tensor(out=to, in0=src, scalar=scale, in1=hi,
                                               op0=ALU.mult, op1=ALU.subtract).then_inc(made, 1)

            def newton_step(n, width):
                nc.vector.tensor_tensor(newton[:, 0:width], rough[:, 0:width], rough[:, 0:width], ALU.mult).then_inc(stats_made, 1)
                dve.wait_ge(stats_made, n + 1)
                nc.vector.tensor_tensor(newton[:, 0:width], newton[:, 0:width], var_eps[:, 0:width], ALU.mult).then_inc(stats_made, 1)
                dve.wait_ge(stats_made, n + 2)
                nc.vector.tensor_scalar(newton[:, 0:width], newton[:, 0:width], -0.5 * H_SCALE, 1.5 * H_SCALE,
                                        ALU.mult, ALU.add).then_inc(stats_made, 1)
                dve.wait_ge(stats_made, n + 3)
                nc.vector.tensor_tensor(rstd[:, 0:width], newton[:, 0:width], rough[:, 0:width], ALU.mult).then_inc(stats_made, 1)
                dve.wait_ge(stats_made, n + 4)

            GROUP_STATS = GT + 1 + 4

            def gather_stats(g, slot):
                for t in range(GT):
                    nc.vector.bn_stats(stats[:, t, :], xg[:, slot, t]).then_inc(stats_made, 1)

            def gather_variances(g):
                for t in range(GT):
                    last = nc.vector.bn_aggr(moments[:, t, :], stats[:, t, :])
                last.then_inc(stats_made, 1)
                dve.wait_ge(stats_made, g * GROUP_STATS + GT + 1)
                nc.vector.tensor_scalar(var_eps[:, :], moments[:, :, 1], EPS, None, ALU.add).then_inc(var_made, 1)

            def normalise(g, slot):
                dve.wait_ge(rough_made, g + 1)
                newton_step(g * GROUP_STATS + GT + 1, GT)
                for t in range(GT):
                    nc.vector.tensor_scalar(hg[:, slot, t], xg[:, slot, t], moments[:, t, 0:1], rstd[:, t:t + 1],
                                            ALU.subtract, ALU.mult).then_inc(h_made, 1)

            def add_logits(g, slot, t):
                wait_from(dve, logits_made, g * GT + t)
                nc.vector.scalar_tensor_tensor(out=node_products, in0=hg[:, slot, t], scalar=0.0, in1=node_w_sb[:, :],
                                               op0=ALU.max, op1=ALU.mult,
                                               accum_out=logits[:, bass.ds(g * GT + t, 1)]).then_inc(logits_made, 1)

            def hT_lo(g, k, slot):
                dve.wait_ge(hT_hi_made, g * KD + k + 1)
                nc.vector.scalar_tensor_tensor(out=hT[:, slot, 1, k], in0=hT_ps[k % 2], scalar=0.0, in1=hT[:, slot, 0, k],
                                               op0=ALU.max, op1=ALU.subtract).then_inc(hT_lo_made, 1)

            def project(g, slot, ahead, x_count):
                first = isinstance(g, int) and g == 0
                for m in range(KD):
                    if ahead and not first:
                        hT_lo(g + 1, m, 1 - slot)
                    dve.wait_ge(g_hi_made, g * KD + m + 1)
                    cols = bass.ds(g * CW, CW)
                    lo_of(gT_lo[:, m, cols], g_ps[m % 2], G_SCALE / (H_SCALE * W_SCALE), gT_hi[:, m, cols], g_lo_made)
                    if first and m == 0:
                        dve.wait_ge(stats_made, GROUP_STATS + GT)
                        gather_variances(1)
                    if first and m == 1:
                        normalise(1, 1)
                    if first and m == 2:
                        dve.wait_ge(node_in, 16)
                        for t in range(GT):
                            add_logits(0, 0, t)
                    if not first:
                        add_logits(g, slot, m)
                if x_count is not None:
                    dve.wait_ge(xg_in[slot], x_count)
                    dve.wait_ge(hT_done, g * KD + KD)
                    gather_stats(g + 2, slot)
                for t in range(GT):
                    if first:
                        hT_lo(1, t, 1)
                    if t == 0 and x_count is not None:
                        dve.wait_ge(stats_made, (g + 2) * GROUP_STATS + GT)
                    dve.wait_ge(s_hi_made, g * GT + t + 1)
                    tile = bass.ds(g * GT + t, 1)
                    lo_of(s_lo[:, tile].rearrange("p o d -> p (o d)"), s_ps[t % 2], S_SCALE / (H_SCALE * W_SCALE),
                          s_hi[:, tile].rearrange("p o d -> p (o d)"), s_lo_made)
                    if t == 0 and x_count is not None:
                        gather_variances(g + 2)
                    if t == 1 and x_count is not None:
                        normalise(g + 2, slot)

            dve.wait_ge(ones_made, 2)
            dve.wait_ge(xg_in[0], 16)
            gather_stats(0, 0)
            dve.wait_ge(stats_made, GT)
            gather_variances(0)
            normalise(0, 0)
            dve.wait_ge(w_hi_made, 1)
            lo_of(edge_hl[:, 1].rearrange("p k n -> p (k n)"), stage_edge, W_SCALE,
                  edge_hl[:, 0].rearrange("p k n -> p (k n)"), w_lo_made)
            for k in range(KD):
                hT_lo(0, k, 0)
            dve.wait_ge(xg_in[1], 16)
            gather_stats(1, 1)
            dve.wait_ge(w_hi_made, 2)
            lo_of(w_hl[:, 1].rearrange("p k n -> p (k n)"), stage_w, W_SCALE,
                  w_hl[:, 0].rearrange("p k n -> p (k n)"), w_lo_made)
            project(0, 0, True, 32)
            dve.wait_ge(w_hi_made, 3)
            lo_of(w1_hl[:, 1].rearrange("p k n -> p (k n)"), stage_w1, W_SCALE,
                  w1_hl[:, 0].rearrange("p k n -> p (k n)"), w_lo_made)
            with dve.Fori(0, (GROUPS - 4) // 2) as s:
                project(s * 2 + 1, 1, True, s * 16 + 32)
                project(s * 2 + 2, 0, True, s * 16 + 48)
            project(GROUPS - 3, 1, True, GROUPS // 2 * 16)
            project(GROUPS - 2, 0, True, None)
            project(GROUPS - 1, 1, False, None)

            dve.wait_ge(logits_made, TILES)
            nc.vector.tensor_reduce(out=node_col[:, :], in_=logits[:, :], axis=AX.X, op=ALU.max).then_inc(node_step, 1)
            dve.wait_ge(node_step, 1)
            nc.vector.tensor_scalar(node_row[:, :], ones[:, :], node_col[:, :], None, ALU.mult).then_inc(node_step, 1)

            COMPARED = {4: (0,), 5: (1, 2), 6: (3, 4), 7: (5, 6), CHUNKS: (7,)}

            def make_penalty(i, c, par):
                if c % 4 == 0:
                    dve.wait_ge(adj_in[par][c // 4], (i - par) * 8 + 16)
                if c - 1 in COMPARED:
                    dve.wait_ge(odd_made, i * CHUNKS + COMPARED[c - 1][-1] + 1)
                wait_from(dve, masked, i * CHUNKS + c - 1)
                nc.vector.tensor_scalar(penalty[:, c % 2], adj_sb[:, par, c * CW:(c + 1) * CW], 0.0,
                                        NEG_BIG * E_SCALE, ALU.is_le, ALU.mult).then_inc(penalty_made, 1)

            def times_adj(i, c, par):
                dve.wait_ge(exp_made, i * CHUNKS + c + 1)
                piece = probs[:, c * CW:(c + 1) * CW]
                nc.vector.tensor_tensor(piece, piece, adj_sb[:, par, c * CW:(c + 1) * CW], ALU.mult).then_inc(probs_made, 1)

            def wait_for_scores(i, row, c):
                if c < row.R:
                    dve.wait_ge(loaded_in[row.loaded_slot(c)], row.loaded_uses(c) * 16 + 16)
                    dve.wait_ge(pT_done, (i - 1) * CHUNKS + c + 1)
                else:
                    dve.wait_ge(score_done, row.computed0 + c - row.R + 1)
                dve.wait_ge(penalty_made, i * CHUNKS + c + 1)

            def compare_adj(i, c, par):
                for k in COMPARED.get(c, ()):
                    dve.wait_ge(adj_16_made, i * CHUNKS + k + 1)
                    dve.wait_ge(masked, i * CHUNKS + c)
                    wait_from(dve, odd_made, i * CHUNKS + k)
                    nc.vector.scalar_tensor_tensor(out=penalty[:, (c + 1) % 2], in0=adj_sb[:, par, k * CW:(k + 1) * CW], scalar=1.0,
                                                   in1=adj_16[:, k // 2 % 2, k % 2 * CW:(k % 2 + 1) * CW], op0=ALU.mult,
                                                   op1=ALU.not_equal, accum_out=odd_chunk[:, k:k + 1]).then_inc(odd_made, 1)

            def pT_lo_of(tile, c):
                dve.wait_ge(pT_hi_made, tile * CHUNKS + c + 1)
                lo_of(pT_lo[:, c % 2].rearrange("p b n -> p (b n)"), pT_ps[c % 2], P_SCALE,
                      pT_hi[:, c % 2].rearrange("p b n -> p (b n)"), pT_lo_made)

            STATS0 = GROUPS * GROUP_STATS
            TILE_STATS = 2 + 4

            def step(i, row=None):
                scores, products, layer1 = parts(i, row)
                par = row.par if row else 0
                first = isinstance(i, int) and i == 0
                last = isinstance(i, int) and i == TILES
                if scores:
                    make_penalty(i, 0, par)
                if last:
                    dve.wait_ge(odd_tile_made, TILES)
                    nc.vector.tensor_reduce(out=odd_row[:, :], in_=odd_tile[:, :], axis=AX.X, op=ALU.add).then_inc(odd_row_made, 1)
                for c in range(CHUNKS):
                    if layer1 and c == 3:
                        dve.wait_ge(stats_made, STATS0 + (i - 2) * TILE_STATS + 1)
                    if scores and c == CHUNKS - 1:
                        wait_for_scores(i, row, c)
                    if products and c > 1:
                        pT_lo_of(i - 1, c)
                    if products and c + AHEAD < CHUNKS:
                        times_adj(i - 1, c + AHEAD, 1 - par)
                    if products and c == 0:
                        pT_lo_of(i - 1, 1)
                    base = STATS0 + (i - 2) * TILE_STATS
                    if layer1 and c == 2:
                        dve.wait_ge(x1_made, i - 1)
                        nc.vector.bn_stats(stats[:, 0, :], x_sb[:, :]).then_inc(stats_made, 1)
                    if layer1 and c == 3:
                        nc.vector.bn_aggr(moments[:, 0, :], stats[:, 0, :]).then_inc(stats_made, 1)
                        dve.wait_ge(stats_made, base + 2)
                        nc.vector.tensor_scalar(var_eps[:, 0:1], moments[:, 0, 1:2], EPS, None, ALU.add).then_inc(var_made, 1)
                    if layer1 and c == 4:
                        dve.wait_ge(rough_made, i - 1 + GROUPS)
                        newton_step(base + 2, 1)
                        wait_from(dve, h1T_done, i - 2)
                        nc.vector.tensor_scalar(h1_sb[:, :], x_sb[:, :], moments[:, 0, 0:1], rstd[:, 0:1],
                                                ALU.subtract, ALU.mult).then_inc(h1_made, 1)
                    if scores:
                        compare_adj(i, c, par)
                    if scores and c < CHUNKS - 1:
                        wait_for_scores(i, row, c)
                        make_penalty(i, c + 1, par)
                    if scores:
                        source = loaded[:, row.loaded_slot(c), :] if c < row.R else score_ps[row.score_bank(c)]
                        nc.vector.tensor_tensor_reduce(probs[:, c * CW:(c + 1) * CW], source, penalty[:, c % 2],
                                                       1.0, -3.0e38, ALU.add, ALU.max,
                                                       chunk_max[:, c:c + 1]).then_inc(masked, 1)
                    if layer1 and c == 6:
                        dve.wait_ge(h1T_hi_made, i - 1)
                        nc.vector.scalar_tensor_tensor(out=h1T[:, 1].rearrange("p k n -> p (k n)"), in0=h1T_ps, scalar=0.0,
                                                       in1=h1T[:, 0].rearrange("p k n -> p (k n)"),
                                                       op0=ALU.max, op1=ALU.subtract).then_inc(h1T_lo_made, 1)
                    if first and c == 2:
                        dve.wait_ge(node_row_done, 1)
                        nc.vector.tensor_reduce(out=node_neg[:, :], in_=y_ps[:, 0:P], axis=AX.X, op=ALU.max,
                                                negate=True).then_inc(node_step, 1)
                        dve.wait_ge(node_step, 3)
                        nc.vector.tensor_scalar(node_neg[:, :], node_neg[:, :], 1.0 / H_SCALE, None, ALU.mult).then_inc(node_step, 1)
                    if last and c == 3:
                        dve.wait_ge(odd_total_done, 1)
                        nc.vector.tensor_scalar(odd_count[:, :], y_ps[:, 0:1], 1.0, None, ALU.mult).then_inc(odd_count_made, 1)
                    if first and c == 6:
                        dve.wait_ge(node_total_done, 1)
                        nc.vector.reciprocal(node_rec[:, :], y_ps[:, 0:1]).then_inc(node_step, 1)
                        dve.wait_ge(node_step, 5)
                        nc.vector.tensor_scalar(node_att[:, :], node_att[:, :], node_rec[:, :], 1.0 / (P_SCALE * S_SCALE),
                                                ALU.mult, ALU.mult).then_inc(node_step, 1)
                if scores:
                    dve.wait_ge(masked, i * CHUNKS + CHUNKS)
                    nc.vector.tensor_reduce(out=row_max[:, :], in_=chunk_max[:, :], axis=AX.X, op=ALU.max).then_inc(max_step, 1)
                    dve.wait_ge(max_step, i * 2 + 1)
                    nc.vector.tensor_scalar(neg_max[:, :], row_max[:, :], -1.0 / E_SCALE, None, ALU.mult).then_inc(max_step, 1)
                    for c in range(AHEAD):
                        times_adj(i, c, par)
                    compare_adj(i, CHUNKS, par)
                if layer1:
                    dve.wait_ge(y_hi_made, i - 1)
                    lo_of(y_out[:, 1] if scores else y_lo[:, i - 2], y_ps, Y_SCALE / (H_SCALE * W_SCALE),
                          y_out[:, 0] if scores else y_hi[:, i - 2], y_lo_made)
                if products:
                    base = (i - 1) * 3
                    if isinstance(i, int) and i == 1:
                        dve.wait_ge(node_step, 6)
                    nc.vector.reduce_sum(out=row_sum[:, :], in_=chunk_sum[:, 1 - par, :], axis=AX.X).then_inc(sum_step, 1)
                    dve.wait_ge(sum_step, base + 1)
                    nc.vector.reciprocal(row_rec[:, :], row_sum[:, :]).then_inc(sum_step, 1)
                    dve.wait_ge(sum_step, base + 2)
                    nc.vector.tensor_tensor(row_fac[:, :], row_rec[:, :], node_att[:, bass.ds(i - 1, 1)], ALU.mult).then_inc(sum_step, 1)
                if scores:
                    pT_lo_of(i, 0)
                    dve.wait_ge(odd_made, i * CHUNKS + CHUNKS)
                    nc.vector.tensor_reduce(out=odd_tile[:, bass.ds(i, 1)], in_=odd_chunk[:, :], axis=AX.X,
                                            op=ALU.add).then_inc(odd_tile_made, 1)
                if products:
                    dve.wait_ge(sum_step, base + 3)
                    dve.wait_ge(xb_made, i)
                    dve.wait_ge(att_done, i * CHUNKS)
                    nc.vector.scalar_tensor_tensor(out=x_sb[:, :], in0=att_ps[1 - par], scalar=row_fac[:, :], in1=x_sb[:, :],
                                                   op0=ALU.mult, op1=ALU.add).then_inc(x1_made, 1)

            steps(dve, step)
            step(TILES)
            step(TILES + 1)

            with dve.Fori(0, GROUPS // 2) as s:
                for slot in range(2):
                    dve.wait_ge(x1_in[slot], s * 16 + 16)
                    for t in range(GT):
                        dve.wait_ge(relu_made, (s * 2 + slot) * GT + t + 1)
                        nc.vector.tensor_tensor(out_grp[:, slot, t], out_grp[:, slot, t], x1_grp[:, slot, t],
                                                ALU.add).then_inc(out_made, 1)

            dve.wait_ge(odd_count_made, 1)
            with dve.If(dve.value_load(odd_count[0:1, 0:1]) > 0):
                dve.wait_ge(z_done, TILES)
                for sl in range(2):
                    dve.wait_ge(out_stored[sl], GROUPS // 2 * GT * 16)
                for h in range(2):
                    rows = slice(h * TILES // 2, (h + 1) * TILES // 2)
                    nc.vector.tensor_tensor(exact_y[h], y_hi[:, rows, :], y_lo[:, rows, :], ALU.add).then_inc(exact_y_made, 1)
                with dve.Fori(0, TILES) as i:
                    dve.wait_ge(exact_x1_in, i * 16 + 16)
                    dve.wait_ge(exact_relu_made, i + 1)
                    nc.vector.tensor_tensor(exact_out, exact_out, exact_x1, ALU.add).then_inc(exact_out_made, 1)
            with dve.Else():
                dve.wait_ge(odd_count_made, 1)

        @block.tensor
        def _(pe):
            def product(bank, stationary, moving, done):
                for k in range(KD):
                    for n, (a, b) in enumerate(((0, 0), (0, 1), (1, 0))):
                        last = nc.tensor.matmul(bank, stationary(a, k), moving(b, k), start=(k == 0 and n == 0),
                                                stop=(k == KD - 1 and n == 2))
                last.then_inc(done, 1)

            def transposed(bank, block_of, done):
                for b in range(BPC):
                    last = nc.tensor.transpose(bank[:, b * P:(b + 1) * P], block_of(b), ident[:, :])
                last.then_inc(done, 1)

            def transpose_h(g, k, slot):
                pe.wait_ge(h_made, g * GT + GT)
                wait_from(pe, hT_lo_made, g * KD + k - 1)
                transposed(hT_ps[k % 2], lambda t: hg[:, slot, t, k * P:(k + 1) * P], hT_done)

            def project(g, slot, ahead):
                first = isinstance(g, int) and g == 0
                for m in range(KD):
                    if ahead and not first:
                        transpose_h(g + 1, m, 1 - slot)
                    if m == 0:
                        pe.wait_ge(hT_lo_made, g * KD + KD)
                    wait_from(pe, g_lo_made, g * KD + m - 1)
                    product(g_ps[m % 2], lambda a, k: edge_hl[:, a, k, m * P:(m + 1) * P],
                            lambda b, k: hT[:, slot, b, k, :], g_done)
                if first:
                    pe.wait_ge(w_lo_made, 2)
                for t in range(GT):
                    if first:
                        transpose_h(1, t, 1)
                    wait_from(pe, s_lo_made, g * GT + t - 1)
                    rows = slice(t * P, (t + 1) * P)
                    product(s_ps[t % 2], lambda a, k: hT[:, slot, a, k, rows], lambda b, k: w_hl[:, b, k, :], s_done)

            pe.wait_ge(ident_made, 2)
            for k in range(KD):
                transpose_h(0, k, 0)
            pe.wait_ge(w_lo_made, 1)
            project(0, 0, True)
            with pe.Fori(0, (GROUPS - 2) // 2) as s:
                project(s * 2 + 1, 1, True)
                project(s * 2 + 2, 0, True)
            project(GROUPS - 1, 1, False)

            def transpose_scores(row, c):
                m = row.moved0 + c - row.R - 1
                pe.wait_ge(raw_made, m + 1)
                wait_from(pe, scoresT_made, m)
                transposed(scoresT_ps, lambda b: raw[:, row.moved_slot(c), b * P:(b + 1) * P], scoresT_done)

            def transpose_h1(tile):
                pe.wait_ge(h1_made, tile + 1)
                wait_from(pe, y_lo_made, tile)
                transposed(h1T_ps, lambda k: h1_sb[:, k * P:(k + 1) * P], h1T_done)

            def make_y(tile):
                pe.wait_ge(h1T_lo_made, tile + 1)
                product(y_ps, lambda a, k: h1T[:, a, k, :], lambda b, k: w1_hl[:, b, k, :], y_done)

            def transpose_probs(tile, c):
                n = tile * CHUNKS + c
                pe.wait_ge(probs_made, n + 1)
                wait_from(pe, pT_lo_made, n - 1)
                transposed(pT_ps[c % 2], lambda b: probs[:, c * CW + b * P:c * CW + (b + 1) * P], pT_done)

            def add_products(i, c, par):
                n = (i - 1) * CHUNKS + c
                pe.wait_ge(pT_lo_made, n + 1)
                if c == 0:
                    wait_from(pe, x1_made, i - 2)
                for b in range(BPC):
                    j = c * BPC + b
                    for m, (pT, s) in enumerate(((pT_hi, s_hi), (pT_hi, s_lo), (pT_lo, s_hi))):
                        last = nc.tensor.matmul(att_ps[1 - par], pT[:, c % 2, b, :], s[:, j, :], start=(j == 0 and m == 0),
                                                stop=(j == TILES - 1 and m == 2))
                last.then_inc(att_done, 1)

            def step(i, row=None):
                scores, products, layer1 = parts(i, row)
                par = row.par if row else 0
                first = isinstance(i, int) and i == 0
                last = isinstance(i, int) and i == TILES
                for c in range(CHUNKS):
                    if products and c != 1:
                        transpose_probs(i - 1, c if c else 1)
                    if scores and c >= row.R:
                        k = c - row.R
                        if k == 0:
                            pe.wait_ge(g_cur_made, i * 2 + 2)
                        wait_from(pe, masked, i * CHUNKS + (c - 1 if k >= 2 else 0))
                        wait_from(pe, raw_made, row.moved0 + (k - 2 if k >= 2 else 0))
                        product(score_ps[row.score_bank(c)], lambda a, k: g_cur[par][:, a, k, :],
                                lambda b, k: (gT_hi, gT_lo)[b][:, k, c * CW:(c + 1) * CW], score_done)
                        if k >= 2:
                            transpose_scores(row, c - 1)
                    if layer1 and c == 6:
                        if last:
                            pe.wait_ge(odd_count_made, 1)
                        transpose_h1(i - 2)
                    if first and c == 0:
                        pe.wait_ge(node_step, 2)
                        nc.tensor.matmul(y_ps[:, 0:P], node_row[:, :], ident[:, :], start=True, stop=True).then_inc(node_row_done, 1)
                    if last and c == 2:
                        pe.wait_ge(odd_row_made, 1)
                        pe.wait_ge(y_lo_made, i - 2)
                        nc.tensor.matmul(y_ps[:, 0:1], ones[:, :], odd_row[:, :], start=True, stop=True).then_inc(odd_total_done, 1)
                    if first and c == 5:
                        pe.wait_ge(node_exp_made, 1)
                        nc.tensor.matmul(y_ps[:, 0:1], ones[:, :], node_sum[:, :], start=True, stop=True).then_inc(node_total_done, 1)
                    if products and c >= 1:
                        add_products(i, c - 1, par)
                if layer1:
                    make_y(i - 2)
                if scores and row.R < CHUNKS - 1:
                    transpose_scores(row, CHUNKS - 1)
                if scores:
                    transpose_probs(i, 0)
                if products:
                    add_products(i, CHUNKS - 1, par)

            pe.wait_ge(s_lo_made, TILES)
            steps(pe, step)
            step(TILES)

            def add_rows(slot, t, blocks):
                for j in blocks:
                    for m, y in enumerate((y_hi, y_lo)):
                        last = nc.tensor.matmul(banks[:, slot * GT + t, :], adjT_grp[slot][:, t, j * P:(j + 1) * P],
                                                y[:, j, :], start=(j == 0 and m == 0), stop=(j == TILES - 1 and m == 1))
                if blocks[-1] == TILES - 1:
                    last.then_inc(z_done, 1)

            pe.wait_ge(y_in_early, (SUPER - 1) * (CHUNKS - 1) * 2 * 16)
            pe.wait_ge(y_in_late, 4 * 16)
            pe.wait_ge(adjT_in_first[0], 16)
            add_rows(0, 0, range(TILES - 2))
            transpose_h1(TILES - 1)
            pe.wait_ge(adjT_in_first[1], 16)
            add_rows(0, 1, range(CHUNKS))
            make_y(TILES - 1)
            add_rows(0, 1, range(CHUNKS, TILES - 2))
            pe.wait_ge(y_lo_made, TILES)
            for t in range(2):
                add_rows(0, t, range(TILES - 2, TILES))
            for t in range(2, GT):
                pe.wait_ge(adjT_in_first[t], 16)
                add_rows(0, t, range(TILES))
            pe.wait_ge(adjT_in[1], GT * 16)
            for t in range(GT):
                add_rows(1, t, range(TILES))
            with pe.Fori(1, GROUPS // 2) as s:
                for slot in range(2):
                    pe.wait_ge(adjT_in[slot], s * (GT * 16) + slot * (GT * 16))
                    pe.wait_ge(relu_made, (s * 2 + slot - 1) * GT)
                    for t in range(GT):
                        add_rows(slot, t, range(TILES))

            pe.wait_ge(odd_count_made, 1)
            with pe.If(pe.value_load(odd_count[0:1, 0:1]) > 0):
                pe.wait_ge(relu_made, TILES)
                pe.wait_ge(exact_y_made, 2)
                with pe.Fori(0, TILES) as i:
                    for c in range(CHUNKS):
                        if c == 0:
                            pe.wait_ge(exact_adj_in, i * 16 + 16)
                        if c >= 2:
                            pe.wait_ge(exact_adjT_made, i * CHUNKS + c - 1)
                        transposed(banks[:, c % 2, :], lambda b: exact_adj[:, c * CW + b * P:c * CW + (b + 1) * P],
                                   exact_adjT_done)
                    pe.wait_ge(exact_adjT_made, i * CHUNKS + CHUNKS)
                    pe.wait_ge(exact_relu_made, i)
                    for j in range(TILES):
                        last = nc.tensor.matmul(banks[:, 2, :], exact_adjT[:, j * P:(j + 1) * P],
                                                exact_y[j // (TILES // 2)][:, j % (TILES // 2), :],
                                                start=(j == 0), stop=(j == TILES - 1))
                    last.then_inc(exact_z_done, 1)
            with pe.Else():
                pe.wait_ge(odd_count_made, 1)


_INS = ["x", "adj", "L0_gnn_weight", "L0_gnn_bias", "L0_gnn_node_w", "L0_gnn_edge_w", "L1_gnn_weight"]


def kernel(**inputs):
    import concourse.bacc as bacc
    from concourse.bass_utils import run_bass_kernel_spmd

    nc = bacc.Bacc("TRN2", target_bir_lowering=False, num_devices=1, dynamic_dma_scratch_size=1024)
    arrays, args = {}, []
    for name in _INS:
        a = np.ascontiguousarray(inputs[name])
        arrays[f"in_{name}"] = a
        args.append(nc.dram_tensor(f"in_{name}", a.shape, mybir.dt.from_np(a.dtype), kind="ExternalInput").ap())
    out = nc.dram_tensor("out", (N, D), mybir.dt.float32, kind="ExternalOutput").ap()
    build_program(nc, *args, out)
    results = run_bass_kernel_spmd(nc, [arrays], core_ids=[0])
    return results.results[0]["out"]
```
